# Optimizing a Trainium2 kernel written in Bass

```python
import numpy as np
import jax
import jax.numpy as jnp

def _softmax(x, axis=-1):
    return jax.nn.softmax(x, axis=axis)

def _gelu(x):
    return jax.nn.gelu(x, approximate=True)

def _silu(x):
    return jax.nn.silu(x)

def _sigmoid(x):
    return jax.nn.sigmoid(x)

def _layernorm(x, axis=-1, eps=1e-05):
    m = jnp.mean(x, axis=axis, keepdims=True)
    v = jnp.var(x, axis=axis, keepdims=True)
    return (x - m) / jnp.sqrt(v + eps)

def _scatter_add(tgt, idx, src, axis=0):
    return tgt.at[idx].add(src)

def _segment_sum(src, seg, n):
    return jax.ops.segment_sum(src, seg, n)
kernel_name = 'mk_flamingo_gated_d1_seqx_r4_394ff0'

def setup_inputs(seed: int=0):
    np.random.seed(seed)
    _w = jnp.asarray

    def _rec_inputs():
        import jax
        import jax.numpy as jnp
        _rk = jax.random.key(seed)
        x = -0.0003929 + 0.9999 * jax.random.normal(jax.random.fold_in(_rk, 1), (16, 128, 1024), jnp.float32)
        _lenS = 128 - jax.random.randint(jax.random.fold_in(_rk, 7), (16,), 0, max(1, 128 // 4) + 1, jnp.int32)
        _lenS2 = 128 - jax.random.randint(jax.random.fold_in(_rk, 8), (16,), 0, max(1, 128 // 4) + 1, jnp.int32)
        _ctx_4096P = jax.random.normal(jax.random.fold_in(_rk, 11), (16, 16, 1024), jnp.float32)
        _ctx_4096c = jax.random.dirichlet(jax.random.fold_in(_rk, 511), 0.3 * jnp.ones((16,), jnp.float32), (16, 128))
        _ctx_4096t = jnp.einsum('bsk,bkd->bsd', _ctx_4096c, _ctx_4096P)
        _ctx_4096t = _ctx_4096t * jax.lax.rsqrt(jnp.mean(jnp.square(_ctx_4096t)) + 1e-12) * 0.953939
        ctx_4096 = 2.81802e-05 + 1.00001 * (_ctx_4096t + 0.3 * jax.random.normal(jax.random.fold_in(_rk, 611), (16, 128, 1024), jnp.float32))
        _g = jax.random.normal(jax.random.fold_in(_rk, 9001), (2, 1), jnp.float32)
        _g = jnp.sign(_g) * jnp.maximum(jnp.abs(_g), 1.0) + (_g == 0) * 1.0
        g_xattn = _g[0]
        g_ffn = _g[1]
        return (x, ctx_4096, g_xattn, g_ffn)
    x, ctx_4096, g_xattn, g_ffn = _rec_inputs()

    def _L0_xattn_setup():
        import jax, jax.numpy as jnp
        import numpy as np
        EPS = 1e-08

        def _cosine_sim(a, b):
            na = jnp.maximum(jnp.sqrt(jnp.sum(a * a, axis=1)), EPS)
            nb = jnp.maximum(jnp.sqrt(jnp.sum(b * b, axis=1)), EPS)
            return jnp.sum(a * b, axis=1) / (na * nb)
        key = jax.random.key(seed)
        k1, k2, k3 = jax.random.split(key, 3)
        B, C, T, O, K = (8, 128, 1024, 128, 3)
        feature = jax.random.normal(k1, (B, C, T), dtype=jnp.float32)
        embedding = jax.random.normal(k2, (B, C, T), dtype=jnp.float32)
        weight = jax.random.normal(k3, (O, C, K), dtype=jnp.float32) * 0.05
        return {'feature': feature, 'embedding': embedding, 'weight': weight}
    _L0_xattn_all = _L0_xattn_setup()
    _L0_xattn_in = {k: v for k, v in _L0_xattn_all.items() if k in ('weight',)}
    del _L0_xattn_all

    def _L0_ffn_setup():
        import jax, jax.numpy as jnp
        import numpy as np
        N_STREAMS = 4
        DIM = 256
        SINKHORN_ITERS = 50
        SINKHORN_TAU = 0.1
        RMS_EPS = 1.1920929e-07

        def sinkhorn_log(logits, num_iters=SINKHORN_ITERS, tau=SINKHORN_TAU):
            Z = logits / tau
            u0 = jnp.zeros(Z.shape[:-1], Z.dtype)
            v0 = jnp.zeros_like(u0)

            def step(carry, _):
                u, v = carry
                u = -jax.nn.logsumexp(Z + v[..., None, :], axis=-1)
                v = -jax.nn.logsumexp(Z + u[..., :, None], axis=-2)
                return ((u, v), None)
            (u, v), _ = jax.lax.scan(step, (u0, v0), None, length=num_iters)
            return jnp.exp(Z + u[..., :, None] + v[..., None, :])
        key = jax.random.key(seed)
        ks = jax.random.split(key, 6)
        B, T = (4, 512)
        n, C = (N_STREAMS, DIM)
        wd = n * C
        x = jax.random.normal(ks[0], (B, T, wd), dtype=jnp.float32)
        W_res = 0.01 * jax.random.normal(ks[1], (n * n, wd), dtype=jnp.float32)
        W_pre = 0.01 * jax.random.normal(ks[2], (n, wd), dtype=jnp.float32)
        W_post = 0.01 * jax.random.normal(ks[3], (n, wd), dtype=jnp.float32)
        H_res_base = jnp.full((n, n), -0.5, dtype=jnp.float32)
        H_res_base = H_res_base.at[jnp.arange(n), jnp.arange(n)].set(0.0)
        H_pre_base = jnp.zeros((n,), dtype=jnp.float32).at[0].set(1.0)
        H_post_base = jnp.zeros((n,), dtype=jnp.float32)
        gate = jnp.array([5.0], dtype=jnp.float32)
        W_branch = 1.0 / np.sqrt(C) * jax.random.normal(ks[4], (C, C), dtype=jnp.float32)
        return {'x': x, 'W_res': W_res, 'W_pre': W_pre, 'W_post': W_post, 'H_res_base': H_res_base, 'H_pre_base': H_pre_base, 'H_post_base': H_post_base, 'gate': gate, 'W_branch': W_branch}
    _L0_ffn_all = _L0_ffn_setup()
    _L0_ffn_in = {k: v for k, v in _L0_ffn_all.items() if k in ('W_res', 'W_pre', 'W_post', 'H_res_base', 'H_pre_base', 'H_post_base', 'gate', 'W_branch')}
    del _L0_ffn_all
    return {'x': x, 'ctx_4096': ctx_4096, 'g_xattn': g_xattn, 'g_ffn': g_ffn, 'L0_xattn_weight': _L0_xattn_in['weight'], 'L0_ffn_W_res': _L0_ffn_in['W_res'], 'L0_ffn_W_pre': _L0_ffn_in['W_pre'], 'L0_ffn_W_post': _L0_ffn_in['W_post'], 'L0_ffn_H_res_base': _L0_ffn_in['H_res_base'], 'L0_ffn_H_pre_base': _L0_ffn_in['H_pre_base'], 'L0_ffn_H_post_base': _L0_ffn_in['H_post_base'], 'L0_ffn_gate': _L0_ffn_in['gate'], 'L0_ffn_W_branch': _L0_ffn_in['W_branch']}

def reference(x, ctx_4096, g_xattn, g_ffn, L0_xattn_weight, L0_ffn_W_res, L0_ffn_W_pre, L0_ffn_W_post, L0_ffn_H_res_base, L0_ffn_H_pre_base, L0_ffn_H_post_base, L0_ffn_gate, L0_ffn_W_branch):
    import jax
    import jax.numpy as jnp

    def _L0_xattn_ref(feature, embedding, weight):
        import jax, jax.numpy as jnp
        import numpy as np
        EPS = 1e-08

        def _cosine_sim(a, b):
            na = jnp.maximum(jnp.sqrt(jnp.sum(a * a, axis=1)), EPS)
            nb = jnp.maximum(jnp.sqrt(jnp.sum(b * b, axis=1)), EPS)
            return jnp.sum(a * b, axis=1) / (na * nb)
        B, C, T = feature.shape
        O = weight.shape[0]
        K = 3
        emb_l = jnp.pad(embedding[:, :, :-1], ((0, 0), (0, 0), (1, 0)))
        emb_r = jnp.pad(embedding[:, :, 1:], ((0, 0), (0, 0), (0, 1)))
        sim = jnp.stack([_cosine_sim(embedding, emb_l), _cosine_sim(embedding, embedding), _cosine_sim(embedding, emb_r)], axis=1)
        att = jnp.repeat(sim, C, axis=1)
        f_pad = jnp.pad(feature, ((0, 0), (0, 0), (1, 1)))
        inp_unf = jnp.stack([f_pad[:, :, k:k + T] for k in range(K)], axis=2)
        inp_unf = inp_unf.reshape(B, C * K, T)
        w_flat = weight.reshape(O, C * K)
        out = jnp.einsum('bit,oi->bot', inp_unf * att, w_flat)
        return out

    def _L0_ffn_ref(x, W_res, W_pre, W_post, H_res_base, H_pre_base, H_post_base, gate, W_branch):
        import jax, jax.numpy as jnp
        import numpy as np
        N_STREAMS = 4
        DIM = 256
        SINKHORN_ITERS = 50
        SINKHORN_TAU = 0.1
        RMS_EPS = 1.1920929e-07

        def sinkhorn_log(logits, num_iters=SINKHORN_ITERS, tau=SINKHORN_TAU):
            Z = logits / tau
            u0 = jnp.zeros(Z.shape[:-1], Z.dtype)
            v0 = jnp.zeros_like(u0)

            def step(carry, _):
                u, v = carry
                u = -jax.nn.logsumexp(Z + v[..., None, :], axis=-1)
                v = -jax.nn.logsumexp(Z + u[..., :, None], axis=-2)
                return ((u, v), None)
            (u, v), _ = jax.lax.scan(step, (u0, v0), None, length=num_iters)
            return jnp.exp(Z + u[..., :, None] + v[..., None, :])
        B, T, nC = x.shape
        n = N_STREAMS
        C = nC // n
        x_norm = x * jax.lax.rsqrt(jnp.mean(x * x, axis=-1, keepdims=True) + RMS_EPS)
        H_res_logits = (x_norm @ W_res.T).reshape(B, T, n, n) + H_res_base
        H_pre_logits = x_norm @ W_pre.T + H_pre_base
        H_post_logits = x_norm @ W_post.T + H_post_base
        H_res = sinkhorn_log(H_res_logits)
        H_pre = jax.nn.softmax(H_pre_logits, axis=-1)
        H_post = jax.nn.softmax(H_post_logits, axis=-1)
        g = jax.nn.sigmoid(gate)[0]
        I = jnp.eye(n, dtype=H_res.dtype)
        H_res = (1.0 - g) * I + g * H_res
        x_streams = x.reshape(B, T, n, C)
        x_pre = jnp.einsum('btnc,btn->btc', x_streams, H_pre)
        y = x_pre @ W_branch
        x_mixed = jnp.einsum('btij,btjc->btic', H_res, x_streams)
        y_distributed = jnp.einsum('btc,btn->btnc', y, H_post)
        return (x_mixed + y_distributed).reshape(B, T, nC)
    x = x + jnp.tanh(g_xattn[0]) * _L0_xattn_ref(_layernorm(x, axis=-1), ctx_4096, L0_xattn_weight)
    x = x + jnp.tanh(g_ffn[0]) * _L0_ffn_ref(_layernorm(x, axis=-1), L0_ffn_W_res, L0_ffn_W_pre, L0_ffn_W_post, L0_ffn_H_res_base, L0_ffn_H_pre_base, L0_ffn_H_post_base, L0_ffn_gate, L0_ffn_W_branch)
    return x

_drawn_inputs = setup_inputs


def setup_inputs(seed=0):
    import zlib

    import numpy as np

    out = dict(_drawn_inputs(seed))
    spreads = {'L0_ffn_H_post_base': (0.0, 0.533)}
    factors = {}
    for name, (base, spread) in spreads.items():
        noise = np.random.default_rng([zlib.crc32(name.encode()), seed]).standard_normal(out[name].shape)
        drawn = base * np.exp(spread * noise) if base else spread * noise
        out[name] = jnp.asarray(drawn.astype(out[name].dtype))
    for name, factor in factors.items():
        out[name] = (out[name] * factor).astype(out[name].dtype)
    return out
```

```python
from contextlib import ExitStack

import concourse.bass as bass
from concourse import mybir

F32 = mybir.dt.float32
BF16 = mybir.dt.bfloat16
ALU = mybir.AluOpType
ACT = mybir.ActivationFunctionType
AX = mybir.AxisListType

P = 128
TAPS = 3
DOTS = 5
PARTS = 3
LN_EPS = 1e-5
RMS_EPS = 1.1920929e-07
COS_EPS = 1e-8
SINKHORN_ITERS = 50
SINKHORN_TAU = 0.1


def at(b, k=1, plus=0):
    reg, off = b
    return reg * (2 * k) + (off * k + plus)


def exists(b, n):
    return not isinstance(b[0], int) or 0 <= b[1] < n


def reused(b, depth):
    return not isinstance(b[0], int) or b[1] >= depth


def ahead(eng, value):
    return value if isinstance(value, int) else eng.snap(value)


def first(b):
    return isinstance(b[0], int) and b[1] == 0


def later(b, d):
    return (b[0], b[1] + d)


def group_of(tap, c):
    return (TAPS * c + tap) // P


def build(nc, x, ctx4, g_xattn, g_ffn, weight, w_res, w_pre, w_post, res_base, pre_base, post_base, gate,
          w_branch, out):
    NB, C, T = x.shape
    NS = pre_base.shape[0]
    DC = T // NS
    NL = NS * NS + 2 * NS
    LP = 32
    NCH = T // P
    H = T // 2
    MIX = (NS + 1) * NS // 2
    QW = T // 4
    assert C == P and H == 512 and NB % 2 == 0 and DC == 2 * P

    with ExitStack() as stack:
        def sb(name, shape, dt=F32):
            return stack.enter_context(nc.sbuf_tensor(name, shape, dt))

        def ps(name, shape, dt=F32):
            return stack.enter_context(nc.psum_tensor(name, shape, dt))

        def sem(name):
            return stack.enter_context(nc.semaphore(name))

        ident = sb("ident", [P, P])
        ident_b = sb("ident_b", [P, P], BF16)
        ones = sb("ones", [P, P])
        unit = sb("unit", [P, DOTS, 32])
        pick = sb("pick", [NCH * 9, NCH, 3], BF16)
        sel = sb("sel", [NCH * 9, NCH, TAPS, P], BF16)
        fold = sb("fold", [P, LP])
        w_nat = sb("w_nat", [P, C * TAPS])
        wg = sb("wg", [P, TAPS, P])
        wl_nat = sb("wl_nat", [LP, T])
        wl = sb("wl", [P, NCH, LP])
        wb = sb("wb", [P, 2, DC])
        row = sb("row", [1, LP])
        crow = sb("crow", [P, LP])
        wsum = sb("wsum", [P, LP])
        gt = sb("gt", [P, 8])
        xs = [sb(f"xs{s}", [P, T]) for s in range(2)]
        es = [sb(f"es{s}", [P, T]) for s in range(2)]
        sq = [sb(f"sq{s}", [P, T + 2]) for s in range(2)]
        pr = [sb(f"pr{s}", [P, T + 2]) for s in range(2)]
        dsb = sb("dsb", [P, QW])
        nm = sb("nm", [P, NCH, 3])
        nq = sb("nq", [P, NCH, 3])
        inv = sb("inv", [P, NCH, 3])
        ww = sb("ww", [P, NCH, 3])
        sims = sb("sims", [P, NCH, 3])
        rest = sb("rest", [P, NCH, 3])
        rest2 = sb("rest2", [P, NCH, 3])
        split = sb("split", [P, NCH, 3, PARTS], BF16)
        rr = [sb(f"rr{s}", [NCH * 9, P], BF16) for s in range(2)]
        bnx = sb("bnx", [P, 2, 6])
        mvx = [sb(f"mvx{s}", [P, 2]) for s in range(2)]
        vex = sb("vex", [P, 1])
        sdx = sb("sdx", [P, 1])
        rsx = sb("rsx", [P, 1])
        ws = [sb(f"ws{s}", [P, TAPS, P]) for s in range(2)]
        gs = [sb(f"gs{k}", [P, T]) for k in range(TAPS)]
        x2 = [sb(f"x2{s}", [P, T]) for s in range(2)]
        bn2 = sb("bn2", [P, NB, 2, 6])
        xt = sb("xt", [P, NCH, P])
        lgs = sb("lgs", [P, P])
        keep = sb("keep", [P, NB, T])
        mv = sb("mv", [P, NB, 2])
        raw = sb("raw", [P, NB, LP])
        ve = sb("ve", [P, NB])
        rstd = sb("rstd", [P, NB])
        rms = sb("rms", [P, NB])
        rs = sb("rs", [P, NB])
        mx = sb("mx", [P, NB, 2])
        logit = sb("logit", [P, NB, NL])
        tmp = sb("tmp", [P, NB, NL])
        z = sb("z", [P, NB, NS, NS])
        zm = sb("zm", [P, NB, NS])
        kk = sb("kk", [P, NB, NS, NS])
        kt = sb("kt", [P, NB, NS, NS])
        ssum = sb("ssum", [P, NB, NS])
        av = sb("av", [P, NB, NS])
        bv = sb("bv", [P, NB, NS])
        ln_ = sb("ln_", [P, NB, NS])
        aij = sb("aij", [P, NB, NS * NS])
        hpp = sb("hpp", [P, NB, 2, NS])
        hsum = sb("hsum", [P, NB, 2])
        bias = sb("bias", [P, NB])
        pbias = sb("pbias", [P, NB])
        coef = [sb(f"coef{s}", [P, 32]) for s in range(2)]
        coefs = sb("coefs", [P, NB, 32])
        xm = [sb(f"xm{s}", [P, T]) for s in range(2)]
        om = [sb(f"om{s}", [P, T]) for s in range(2)]
        dg = [sb(f"dg{s}", [P, NS // 2, NS + 1, P]) for s in range(2)]
        xp = sb("xp", [P, DC])
        xpt = sb("xpt", [P, 2, P])
        ys = [sb(f"ys{s}", [P, DC]) for s in range(2)]

        DT = ps("DT", [P, 512])
        MISC = ps("MISC", [P, 512])
        ATT = [ps(f"ATT{k}", [P, 512]) for k in range(TAPS)]
        CV = [ps(f"CV{h}", [P, 512]) for h in range(2)]
        XT = ps("XT", [P, 512])
        DTT = MISC[:, 0:2 * P]
        RP = MISC[0:NCH * 9, 2 * P:2 * P + P // 2].bitcast(BF16)
        LGP = DT[:, QW:QW + P]
        LG = XT[:, 0:LP]

        names = """wlz cdma ident unit pick sel wnat wl1 wlt wlc wgt cro crs tan tanv wgv fld padz con
            sq pr dots dsb dT nm nq inv ww sims hi res mid split RP rr att g bnx mvx vex sdx rsx ws conv x2
            bn2 mv XT xt LGP lgs LG raw v1 a1 v2 sink0 sink1 ch
            mix pre1 pre xpT xpt y ysb coef seen mixd dg mixt mixo"""
        S = {n: sem("s_" + n) for n in names.split()}
        ein = [sem(f"s_ein{s}") for s in range(2)]
        xin = [sem(f"s_xin{s}") for s in range(2)]
        kept = [sem(f"s_kept{s}") for s in range(2)]
        xmin = [sem(f"s_xmin{s}") for s in range(2)]
        outd = [sem(f"s_outd{s}") for s in range(2)]

        block = stack.enter_context(nc.Block())

        def steps(eng, step):
            for t in range(-2, 2):
                step((0, t))
            with eng.Fori(1, NB // 2 - 1) as i:
                step((i, 0))
                step((i, 1))
            for t in range(NB - 2, NB + 1):
                step((0, t))

        @block.sync
        def _(sp):
            def load_e(b):
                n = ahead(sp, at(b))
                if reused(b, 2):
                    sp.wait_ge(S["sq"], at(b, 1, -1))
                    sp.wait_ge(S["pr"], at(b, 1, -1))
                sp.dma_start(es[b[1] % 2][:], ctx4[bass.ds(n, 1)].rearrange("a c t -> (a c) t")
                             ).then_inc(ein[b[1] % 2], 16)

            def load_x(b):
                sp.dma_start(xs[b[1] % 2][:], x[bass.ds(at(b), 1)].rearrange("a c t -> (a c) t")
                             ).then_inc(xin[b[1] % 2], 16)

            def keep_x2(b):
                n = ahead(sp, at(b))
                sp.wait_ge(S["x2"], at(b, 2, 2))
                sp.dma_start(keep[:, bass.ds(n, 1), :].rearrange("p a t -> p (a t)"), x2[b[1] % 2][:]
                             ).then_inc(kept[b[1] % 2], 16)

            def step(u):
                load_e(later(u, 2))
                keep_x2(u)
                load_x(later(u, 2))

            load_e((0, 0))
            load_x((0, 0))
            sp.dma_start(w_nat[:], weight.rearrange("o c k -> o (c k)")).then_inc(S["wnat"], 16)
            sp.dma_start(row[:, 0:16], res_base.rearrange("(a i) j -> a (i j)", a=1)).then_inc(S["cdma"], 16)
            sp.dma_start(row[:, 16:20], pre_base.rearrange("(a i) -> a i", a=1)).then_inc(S["cdma"], 16)
            sp.dma_start(row[:, 20:24], post_base.rearrange("(a i) -> a i", a=1)).then_inc(S["cdma"], 16)
            sp.dma_start(row[:, 24:25], g_xattn.rearrange("(a i) -> a i", a=1)).then_inc(S["cdma"], 16)
            sp.dma_start(row[:, 25:26], g_ffn.rearrange("(a i) -> a i", a=1)).then_inc(S["cdma"], 16)
            sp.dma_start(row[:, 26:27], gate.rearrange("(a i) -> a i", a=1)).then_inc(S["cdma"], 16)
            load_e((0, 1))
            load_x((0, 1))
            sp.wait_ge(S["wlz"], 1)
            sp.dma_start(wl_nat[0:16, :], w_res).then_inc(S["wl1"], 16)
            sp.dma_start(wl_nat[16:20, :], w_pre).then_inc(S["wl1"], 16)
            sp.dma_start(wl_nat[20:24, :], w_post).then_inc(S["wl1"], 16)
            sp.dma_start(wb[:], w_branch.rearrange("(k c) n -> c k n", c=P)).then_inc(S["wl1"], 16)
            for u in range(0, 2):
                step((0, u))
            with sp.Fori(1, NB // 2 - 1) as i:
                step((i, 0))
                step((i, 1))
            for u in (NB - 2, NB - 1):
                keep_x2((0, u))

            def load_m(b):
                n = ahead(sp, at(b))
                if reused(b, 2):
                    sp.wait_ge(S["mixd"], at(b, MIX, -MIX))
                    sp.sem_inc(S["seen"], 1)
                    sp.wait_ge(S["mixt"], at(b, 1, -1))
                    sp.sem_inc(S["seen"], 1)
                sp.dma_start(xm[b[1] % 2][:], keep[:, bass.ds(n, 1), :].rearrange("p a t -> p (a t)")
                             ).then_inc(xmin[b[1] % 2], 16)

            def store(b):
                n = ahead(sp, at(b))
                sp.wait_ge(S["mixd"], at(b, MIX, MIX))
                sp.sem_inc(S["seen"], 1)
                sp.wait_ge(S["mixo"], at(b, 2, 2))
                sp.sem_inc(S["seen"], 1)
                sp.dma_start(out[bass.ds(n, 1)].rearrange("a c t -> (a c) t"), om[b[1] % 2][:]
                             ).then_inc(outd[b[1] % 2], 16)

            sp.wait_ge(kept[0], 16 * NB // 2)
            sp.wait_ge(kept[1], 16 * NB // 2)
            load_m((0, 0))
            load_m((0, 1))
            with sp.Fori(0, NB // 2 - 1) as i:
                for s in range(2):
                    store((i, s))
                    load_m((i, s + 2))
            store((0, NB - 2))
            store((0, NB - 1))
            for s in range(2):
                sp.wait_ge(outd[s], 16 * NB // 2)

        def mix_streams(eng, b, streams, chain):
            s = b[1] % 2
            eng.wait_ge(xmin[s], at((b[0], b[1] // 2 * 2), 8, 16))
            eng.wait_ge(S["coef"], at(b, 1, 1))
            if reused(b, 2):
                eng.wait_ge(outd[s], at((b[0], b[1] // 2 * 2), 8))
            for j in range(NS + 1):
                for n, i in enumerate(streams):
                    o = om[s][:, i * DC:(i + 1) * DC]
                    if j == 0:
                        ins = eng.tensor_scalar(o, xm[s][:, 0:DC], coef[s][:, NS * i:NS * i + 1],
                                                coef[s][:, 24 + i:25 + i], ALU.mult, ALU.add)
                    else:
                        if j == NS and n == 0:
                            eng.wait_ge(S["ysb"], at(b, 1, 1))
                        eng.wait_ge(chain, at(b, MIX, len(streams) * (j - 1) + n + 1))
                        src = xm[s][:, j * DC:(j + 1) * DC] if j < NS else ys[s][:]
                        c = NS * i + j if j < NS else 16 + i
                        ins = eng.scalar_tensor_tensor(out=o, in0=src, scalar=coef[s][:, c:c + 1], in1=o,
                                                       op0=ALU.mult, op1=ALU.add)
                    ins.then_inc(chain, 1)

        @block.gpsimd
        def _(pool):
            pool.memset(wl_nat[:], 0.0).then_inc(S["wlz"], 1)
            pool.memset(ident[:], 0.0).then_inc(S["ident"], 1)
            pool.memset(ones[:], 1.0).then_inc(S["ident"], 1)
            pool.wait_ge(S["ident"], 2)
            pool.affine_select(out=ident[:], in_=ident[:], compare_op=ALU.not_equal, fill=1.0, base=0,
                               pattern=[[-1, P]], channel_multiplier=1).then_inc(S["ident"], 1)
            pool.memset(unit[:], 0.0).then_inc(S["unit"], 1)
            pool.wait_ge(S["unit"], 1)
            for m in range(DOTS):
                pool.memset(unit[:, m, m:m + 1], 1.0).then_inc(S["unit"], 1)
            for s in range(2):
                pool.memset(sq[s][:, 0:1], 0.0).then_inc(S["padz"], 1)
                pool.memset(sq[s][:, T + 1:T + 2], 0.0).then_inc(S["padz"], 1)
                pool.memset(pr[s][:, 0:1], 0.0).then_inc(S["padz"], 1)
                pool.memset(pr[s][:, T:T + 2], 0.0).then_inc(S["padz"], 1)
            pool.memset(gs[0][:, 0:1], 0.0).then_inc(S["padz"], 1)
            pool.memset(gs[2][:, T - 1:T], 0.0).then_inc(S["padz"], 1)
            pool.memset(pick[:], 1.0).then_inc(S["pick"], 1)
            pool.wait_ge(S["pick"], 1)
            pool.affine_select(out=pick[:], in_=pick[:], compare_op=ALU.is_ge, fill=0.0, base=0,
                               pattern=[[-9, NCH], [-3, 3]], channel_multiplier=1).then_inc(S["pick"], 1)
            pool.wait_ge(S["pick"], 2)
            pool.affine_select(out=pick[:], in_=pick[:], compare_op=ALU.is_ge, fill=0.0, base=2,
                               pattern=[[9, NCH], [3, 3]], channel_multiplier=-1).then_inc(S["pick"], 1)
            pool.memset(fold[:], 0.0).then_inc(S["fld"], 1)
            for g in range(4):
                pool.wait_ge(S["fld"], g + 1)
                pool.affine_select(out=fold[:], in_=fold[:], compare_op=ALU.not_equal, fill=1.0, base=-32 * g,
                                   pattern=[[-1, LP]], channel_multiplier=1).then_inc(S["fld"], 1)

            def products(b):
                s = b[1] % 2
                pool.wait_ge(ein[s], at((b[0], b[1] // 2 * 2), 8, 16))
                if reused(b, 2):
                    pool.wait_ge(S["dots"], at(b, 1, -1))
                pool.tensor_tensor(pr[s][:, 1:T], es[s][:, 1:T], es[s][:, 0:T - 1], ALU.mult
                                   ).then_inc(S["pr"], 1)

            one3 = ones[:, 0:3 * NCH].rearrange("p (q m) -> p q m", m=3)

            def split3(b):
                pool.wait_ge(S["sims"], at(b, 2, 2))
                if reused(b, 1):
                    pool.wait_ge(S["RP"], at(b))
                pool.tensor_tensor(split[:, :, :, 0], sims[:], one3, ALU.mult).then_inc(S["hi"], 1)
                pool.wait_ge(S["hi"], at(b, 1, 1))
                pool.tensor_tensor(rest[:], sims[:], split[:, :, :, 0], ALU.subtract).then_inc(S["res"], 1)
                pool.wait_ge(S["res"], at(b, 1, 1))
                pool.tensor_tensor(split[:, :, :, 1], rest[:], one3, ALU.mult).then_inc(S["mid"], 1)
                pool.wait_ge(S["mid"], at(b, 1, 1))
                pool.tensor_tensor(split[:, :, :, 2], rest[:], split[:, :, :, 1], ALU.subtract
                                   ).then_inc(S["split"], 1)

            def step(t):
                if exists(later(t, 2), NB):
                    products(later(t, 2))
                if exists(later(t, 1), NB):
                    split3(later(t, 1))

            steps(pool, step)

            def diagonals(b):
                s = b[1] % 2
                pool.wait_ge(S["coef"], at(b, 1, 1))
                if reused(b, 2):
                    pool.wait_ge(S["mixt"], at(b, 1, -1))
                for n in range(NS // 2):
                    for j in range(NS + 1):
                        i = NS // 2 + n
                        c = NS * i + j if j < NS else 16 + i
                        if n == j == 0:
                            ins = pool.tensor_tensor(dg[s][:, n, j, :], ident[:],
                                                     coef[s][:, c:c + 1].broadcast_to([P, P]), ALU.mult)
                        else:
                            ins = pool.tensor_scalar(dg[s][:, n, j, :], ident[:], coef[s][:, c:c + 1], 0.0,
                                                     ALU.mult, ALU.add)
                        ins.then_inc(S["dg"], 1)

            diagonals((0, 0))
            diagonals((0, 1))
            with pool.Fori(1, NB // 2) as i:
                diagonals((i, 0))
                diagonals((i, 1))

        @block.scalar
        def _(act):
            act.wait_ge(S["ident"], 3)
            act.activation(ident_b[:], ident[:], ACT.Copy).then_inc(S["con"], 1)
            act.wait_ge(S["crs"], 1)
            act.activation(gt[:, 0:2], crow[:, 24:26], ACT.Tanh).then_inc(S["tan"], 1)
            act.activation(gt[:, 4:5], crow[:, 26:27], ACT.Exp, scale=-1.0).then_inc(S["tan"], 1)

            def square(b):
                s = b[1] % 2
                act.wait_ge(ein[s], at((b[0], b[1] // 2 * 2), 8, 16))
                if reused(b, 2):
                    act.wait_ge(S["dots"], at(b, 1, -1))
                act.activation(sq[s][:, 1:T + 1], es[s][:], ACT.Square).then_inc(S["sq"], 1)

            def dots_out(b):
                act.wait_ge(S["dots"], at(b, 1, 1))
                if reused(b, 1):
                    act.wait_ge(S["dT"], at(b))
                act.activation(dsb[:], DT[:, 0:QW], ACT.Copy).then_inc(S["dsb"], 1)

            def sqrt_x(b):
                act.wait_ge(S["vex"], at(b, 1, 1))
                act.activation(sdx[:], vex[:], ACT.Sqrt).then_inc(S["sdx"], 1)

            def sqrt_sims(b):
                act.wait_ge(S["nm"], at(b, 1, 1))
                act.activation(nq[:], nm[:], ACT.Sqrt).then_inc(S["nq"], 1)

            def xt_out(b, h):
                act.wait_ge(S["XT"], at(b, 2, 1 + h))
                if h == 0 and reused(b, 1):
                    act.wait_ge(S["LGP"], at(b))
                act.activation(xt[:, 4 * h:4 * h + 4, :], XT[:].rearrange("p (a c) -> p a c", a=4), ACT.Copy
                               ).then_inc(S["xt"], 1)

            def lgp_out(b):
                act.wait_ge(S["LGP"], at(b, 1, 1))
                act.activation(lgs[:], LGP, ACT.Copy).then_inc(S["lgs"], 1)

            def rr_out(b):
                act.wait_ge(S["RP"], at(b, 1, 1))
                if reused(b, 2):
                    act.wait_ge(S["att"], at(b, 6, -6))
                act.activation(rr[b[1] % 2][:], RP, ACT.Copy).then_inc(S["rr"], 1)

            def lg_out(b):
                act.wait_ge(S["LG"], at(b, 1, 1))
                act.activation(raw[:, bass.ds(at(b), 1), :].rearrange("p a l -> p (a l)"), LG, ACT.Copy
                               ).then_inc(S["raw"], 1)

            def step(t):
                f, n, l = later(t, 2), later(t, 1), later(t, -1)
                if exists(f, NB):
                    square(f)
                if exists(n, NB):
                    dots_out(n)
                    sqrt_x(n)
                if exists(l, NB):
                    xt_out(l, 0)
                if exists(n, NB):
                    sqrt_sims(n)
                if exists(l, NB):
                    xt_out(l, 1)
                    lgp_out(l)
                if exists(n, NB):
                    rr_out(n)
                if exists(l, NB):
                    lg_out(l)

            steps(act, step)

            act.wait_ge(S["v1"], 1)
            act.activation(rstd[:], ve[:], ACT.Sqrt).then_inc(S["a1"], 1)
            act.wait_ge(S["v1"], 2)
            act.activation(rs[:], rms[:], ACT.Sqrt).then_inc(S["a1"], 1)
            act.wait_ge(S["v1"], 3)
            act.activation(hpp[:], hpp[:], ACT.Exp).then_inc(S["a1"], 1)
            act.activation(kk[:], z[:], ACT.Exp).then_inc(S["a1"], 1)
            act.activation(bv[:], zm[:], ACT.Exp).then_inc(S["a1"], 1)
            act.wait_ge(S["v1"], 4)
            act.activation(av[:], av[:], ACT.Ln).then_inc(S["a1"], 1)
            act.activation(ln_[:], bv[:], ACT.Ln).then_inc(S["a1"], 1)
            act.wait_ge(S["v1"], 5)
            act.activation(kk[:], z[:], ACT.Exp).then_inc(S["a1"], 1)

            act.wait_ge(S["v1"], 6)

            def coef_out(b):
                if reused(b, 2):
                    act.wait_ge(S["mixd"], at(b, MIX, -MIX))
                    act.wait_ge(S["dg"], at(b, MIX, -MIX))
                    act.wait_ge(S["mixo"], at(b, 2, -2))
                act.activation(coef[b[1] % 2][:], coefs[:, bass.ds(at(b), 1), :].rearrange("p a l -> p (a l)"),
                               ACT.Copy).then_inc(S["coef"], 1)

            def branch_out(b):
                act.wait_ge(S["xpT"], at(b, 1, 1))
                act.activation(xpt[:], XT[:, 0:2 * P].rearrange("p (a c) -> p a c", a=2), ACT.Copy
                               ).then_inc(S["xpt"], 1)
                act.wait_ge(S["y"], at(b, 1, 1))
                act.activation(ys[b[1] % 2][:], DT[:, 0:DC], ACT.Copy).then_inc(S["ysb"], 1)

            def mix_out(b):
                s = b[1] % 2
                act.wait_ge(S["mixt"], at(b, 1, 1))
                if reused(b, 2):
                    act.wait_ge(outd[s], at((b[0], b[1] // 2 * 2), 8))
                for n in range(NS // 2):
                    i = NS // 2 + n
                    act.activation(om[s][:, i * DC:(i + 1) * DC], CV[s][:, n * DC:(n + 1) * DC], ACT.Identity,
                                   bias=coef[s][:, 24 + i:25 + i]).then_inc(S["mixo"], 1)

            coef_out((0, 0))
            coef_out((0, 1))
            branch_out((0, 0))
            branch_out((0, 1))
            mix_out((0, 0))
            with act.Fori(1, NB // 2) as i:
                coef_out((i, 0))
                branch_out((i, 0))
                mix_out((i, -1))
                coef_out((i, 1))
                branch_out((i, 1))
                mix_out((i, 0))
            mix_out((0, NB - 1))

        @block.tensor
        def _(pe):
            pe.wait_ge(S["ident"], 3)
            pe.wait_ge(S["cdma"], 6 * 16)
            pe.matmul(XT[:, 0:27], ones[0:1, :], row[0:1, 0:27], start=True, stop=True).then_inc(S["cro"], 1)
            pe.wait_ge(S["wnat"], 16)
            wv = w_nat[:].rearrange("o (c k) -> o k c", k=TAPS)
            for k in range(TAPS):
                pe.transpose(CV[0][:, k * P:(k + 1) * P], wv[:, k, :], ident[:]).then_inc(S["wgt"], 1)

            def logit_weights():
                pe.wait_ge(S["wl1"], 64)
                pe.wait_ge(S["crs"], 1)
                for j in range(NCH):
                    pe.transpose(XT[:, 64 + j * LP:64 + (j + 1) * LP], wl_nat[:, j * P:(j + 1) * P],
                                 ident[0:LP, 0:LP]).then_inc(S["wlt"], 1)
                pe.wait_ge(S["wlc"], 1)
                for j in range(NCH):
                    i = pe.matmul(XT[:, 0:LP], ones[:], wl[:, j, :], start=(j == 0), stop=(j == NCH - 1))
                i.then_inc(S["wlt"], 1)

            def dots(b):
                s = b[1] % 2
                pe.wait_ge(S["sq"], at(b, 1, 1))
                pe.wait_ge(S["pr"], at(b, 1, 1))
                if reused(b, 1):
                    pe.wait_ge(S["dsb"], at(b))
                if reused(b, 3):
                    pe.wait_ge(S["lgs"], at(b, 1, -2))
                for m, (src, d) in enumerate(((sq, 0), (sq, 1), (sq, 2), (pr, 0), (pr, 1))):
                    for q in range(4):
                        i = pe.matmul(DT[32 * q:32 * q + 32, 0:QW], unit[:, m, :],
                                      src[s][:, q * QW + d:(q + 1) * QW + d], start=(m == 0),
                                      stop=(m == DOTS - 1), tile_position=(0, 32 * q))
                i.then_inc(S["dots"], 1)

            def dots_turn(b):
                pe.wait_ge(S["dsb"], at(b, 1, 1))
                if reused(b, 1):
                    pe.wait_ge(S["rr"], at(b))
                for r in range(2):
                    i = pe.transpose(DTT[:, r * P:(r + 1) * P], dsb[:, r * P:(r + 1) * P], ident[:])
                i.then_inc(S["dT"], 1)

            def sims_turn(b):
                pe.wait_ge(S["split"], at(b, 1, 1))
                if reused(b, 1):
                    pe.wait_ge(S["rr"], at(b))
                pe.transpose(RP, split[:].rearrange("p a b c -> p (a b c)"), ident_b[:]).then_inc(S["RP"], 1)

            def spread(b, h, k):
                s = b[1] % 2
                if h == 0 and k == 0:
                    pe.wait_ge(S["rr"], at(b, 1, 1))
                if h or reused(b, 1):
                    pe.wait_ge(S["g"], at(b, 6, 3 * h + k + 1 - 3))
                for q in range(NCH // 2):
                    i = pe.matmul(ATT[k][:, q * P:(q + 1) * P], sel[:, 4 * h + q, k, :], rr[s][:],
                                  start=True, stop=True)
                i.then_inc(S["att"], 1)

            def conv(b, h, k):
                s = b[1] % 2
                if h == 0 and k == 0:
                    pe.wait_ge(S["ws"], at(b, 1, 1))
                if k == 0 and reused(b, 1):
                    pe.wait_ge(S["x2"], at(b, 2, h - 1))
                pe.wait_ge(S["g"], at(b, 6, 3 * h + k + 1))
                pe.matmul(CV[h][:], ws[s][:, k, :], gs[k][:, h * H:(h + 1) * H], start=(k == 0),
                          stop=(k == TAPS - 1)).then_inc(S["conv"], 1)

            def x2_turn(b, h):
                s = b[1] % 2
                if h == 0:
                    pe.wait_ge(S["x2"], at(b, 2, 2))
                if first(b) and h == 0:
                    pe.wait_ge(S["wlc"], 2)
                if h:
                    pe.wait_ge(S["xt"], at(b, 2, 1))
                elif reused(b, 1):
                    pe.wait_ge(S["raw"], at(b))
                for q in range(4):
                    j = 4 * h + q
                    i = pe.transpose(XT[:, q * P:(q + 1) * P], x2[s][:, j * P:(j + 1) * P], ident[:])
                i.then_inc(S["XT"], 1)

            def logits(b):
                pe.wait_ge(S["xt"], at(b, 2, 2))
                if reused(b, 1):
                    pe.wait_ge(S["lgs"], at(b))
                pe.wait_ge(S["dsb"], min(b[1] + 3, NB) if isinstance(b[0], int) else at(b, 1, 3))
                for r in range(2):
                    for g in range(4):
                        j = 4 * r + g
                        i = pe.matmul(LGP[32 * g:32 * g + 32, :], wl[:, j, :], xt[:, j, :], start=(r == 0),
                                      stop=(r == 1), tile_position=(0, 32 * g))
                i.then_inc(S["LGP"], 1)

            def logits_turn(b):
                pe.wait_ge(S["lgs"], at(b, 1, 1))
                if reused(b, 1):
                    pe.wait_ge(S["raw"], at(b))
                pe.matmul(LG, lgs[:], fold[:], start=True, stop=True).then_inc(S["LG"], 1)

            def step(t):
                n, l = later(t, 1), later(t, -1)
                if first(t):
                    logit_weights()
                if exists(t, NB):
                    for k in range(TAPS):
                        spread(t, 0, k)
                if exists(n, NB):
                    dots(n)
                if exists(t, NB):
                    for k in range(TAPS):
                        spread(t, 1, k)
                        conv(t, 0, k)
                if exists(n, NB):
                    dots_turn(n)
                if exists(l, NB):
                    x2_turn(l, 0)
                if exists(t, NB):
                    for k in range(TAPS):
                        conv(t, 1, k)
                if exists(l, NB):
                    x2_turn(l, 1)
                    logits(l)
                if exists(n, NB):
                    sims_turn(n)
                if exists(l, NB):
                    logits_turn(l)

            pe.wait_ge(S["con"], 1)
            pe.wait_ge(S["unit"], 1 + DOTS)
            pe.wait_ge(S["padz"], 10)
            pe.wait_ge(S["sel"], 9)
            pe.wait_ge(S["fld"], 5)
            steps(pe, step)

            def branch(b):
                pe.wait_ge(S["pre"], at(b, NS, NS))
                if reused(b, 1):
                    pe.wait_ge(S["ysb"], at(b))
                for r in range(2):
                    i = pe.transpose(XT[:, r * P:(r + 1) * P], xp[:, r * P:(r + 1) * P], ident[:])
                i.then_inc(S["xpT"], 1)
                pe.wait_ge(S["xpt"], at(b, 1, 1))
                for r in range(2):
                    i = pe.matmul(DT[:, 0:DC], xpt[:, r, :], wb[:, r, :], start=(r == 0), stop=(r == 1))
                i.then_inc(S["y"], 1)

            def mix(b):
                s = b[1] % 2
                pe.wait_ge(S["dg"], at(b, MIX, MIX))
                if reused(b, 2):
                    pe.wait_ge(S["mixo"], at(b, 2, -2))
                for n in range(NS // 2):
                    for j in range(NS + 1):
                        if n == 0 and j == NS:
                            pe.wait_ge(S["ysb"], at(b, 1, 1))
                        src = xm[s][:, j * DC:(j + 1) * DC] if j < NS else ys[s][:]
                        i = pe.matmul(CV[s][:, n * DC:(n + 1) * DC], dg[s][:, n, j, :], src,
                                      start=(j == 0), stop=(j == NS))
                i.then_inc(S["mixt"], 1)

            branch((0, 0))
            branch((0, 1))
            mix((0, 0))
            with pe.Fori(1, NB // 2) as i:
                branch((i, 0))
                mix((i, -1))
                branch((i, 1))
                mix((i, 0))
            mix((0, NB - 1))

        @block.vector
        def _(dve):
            dve.wait_ge(S["pick"], 3)
            for k in range(TAPS):
                edges = [min(c for c in range(C) if group_of(k, c) == g) for g in range(3)] + [C]
                for g in range(3):
                    n = edges[g + 1] - edges[g]
                    dve.tensor_copy(sel[:, :, k, edges[g]:edges[g + 1]],
                                    pick[:, :, g:g + 1].broadcast_to([NCH * 9, NCH, n])
                                    ).then_inc(S["sel"], 1)
            dve.wait_ge(S["cro"], 1)
            dve.tensor_copy(crow[:, 0:27], XT[:, 0:27]).then_inc(S["crs"], 1)
            dve.wait_ge(S["tan"], 2)
            dve.wait_ge(S["wgt"], 3)
            dve.tensor_scalar(wg[:].rearrange("p k o -> p (k o)"), CV[0][:, 0:TAPS * P], gt[:, 0:1], None,
                              ALU.mult).then_inc(S["wgv"], 1)
            dve.tensor_scalar(gt[:, 5:6], gt[:, 4:5], 1.0, None, ALU.add).then_inc(S["tanv"], 1)
            dve.wait_ge(S["tanv"], 1)
            dve.reciprocal(gt[:, 2:3], gt[:, 5:6]).then_inc(S["tanv"], 1)
            dve.wait_ge(S["tanv"], 2)
            dve.tensor_scalar(gt[:, 3:4], gt[:, 2:3], -1.0, 1.0, ALU.mult, ALU.add).then_inc(S["tanv"], 1)
            dve.wait_ge(S["tanv"], 3)
            dve.wait_ge(S["wgv"], 1)

            def logit_weights():
                dve.wait_ge(S["wlt"], NCH)
                dve.tensor_copy(wl[:], XT[:, 64:64 + NCH * LP].rearrange("p (j l) -> p j l", j=NCH)
                                ).then_inc(S["wlc"], 1)
                dve.wait_ge(S["wlt"], NCH + 1)
                dve.tensor_copy(wsum[:], XT[:, 0:LP]).then_inc(S["wlc"], 1)

            def scale_x(b, h, k):
                s = b[1] % 2
                lo, hi = h * H, (h + 1) * H
                t0, t1 = max(lo, 1 - k), min(hi, T + 1 - k)
                if h == 0 and k == 0:
                    dve.wait_ge(S["mvx"], at(b, 1, 1))
                dve.wait_ge(S["att"], at(b, 6, 3 * h + k + 1))
                if reused(b, 1):
                    dve.wait_ge(S["conv"], at(b, 6, 3 * h + k + 1 - 6))
                dve.scalar_tensor_tensor(out=gs[k][:, t0:t1], in0=xs[s][:, t0 + k - 1:t1 + k - 1],
                                         scalar=mvx[s][:, 0:1], in1=ATT[k][:, t0 - lo:t1 - lo],
                                         op0=ALU.subtract, op1=ALU.mult).then_inc(S["g"], 1)

            def stats_x(b):
                s = b[1] % 2
                dve.wait_ge(xin[s], at((b[0], b[1] // 2 * 2), 8, 16))
                for h in range(2):
                    dve.bn_stats(bnx[:, h, :], xs[s][:, h * H:(h + 1) * H]).then_inc(S["bnx"], 1)
                dve.wait_ge(S["bnx"], at(b, 2, 2))

            def aggregate_x(b):
                s = b[1] % 2
                dve.bn_aggr(mvx[s][:], bnx[:]).then_inc(S["mvx"], 1)
                dve.wait_ge(S["mvx"], at(b, 1, 1))
                dve.tensor_scalar(vex[:], mvx[s][:, 1:2], LN_EPS, None, ALU.add).then_inc(S["vex"], 1)

            def scale_w(b):
                s = b[1] % 2
                dve.wait_ge(S["sdx"], at(b, 1, 1))
                dve.reciprocal(rsx[:], sdx[:]).then_inc(S["rsx"], 1)
                dve.wait_ge(S["rsx"], at(b, 1, 1))
                if reused(b, 2):
                    dve.wait_ge(S["conv"], at(b, 6, -6))
                dve.tensor_scalar(ws[s][:], wg[:], rsx[:, 0:1], None, ALU.mult).then_inc(S["ws"], 1)

            sums = DTT.rearrange("p (r q m) -> p q r m", r=2, q=4)

            def norms(b):
                dve.wait_ge(S["dT"], at(b, 1, 1))
                if reused(b, 1):
                    dve.wait_ge(S["nq"], at(b))
                dve.tensor_scalar(nm[:].rearrange("p (q r) m -> p q r m", r=2), sums[:, :, :, 0:3],
                                  COS_EPS * COS_EPS, None, ALU.max).then_inc(S["nm"], 1)

            def norms2(b):
                dve.wait_ge(S["nq"], at(b, 1, 1))
                dve.reciprocal(inv[:], nq[:]).then_inc(S["inv"], 1)

            def norms3(b):
                dve.wait_ge(S["inv"], at(b, 1, 1))
                dve.tensor_tensor(ww[:], inv[:], inv[:, :, 1:2].broadcast_to([P, NCH, 3]), ALU.mult
                                  ).then_inc(S["ww"], 1)

            def cosines(b):
                dve.wait_ge(S["ww"], at(b, 1, 1))
                if reused(b, 1):
                    dve.wait_ge(S["split"], at(b))
                wv = ww[:].rearrange("p (q r) m -> p q r m", r=2)
                sv = sims[:].rearrange("p (q r) m -> p q r m", r=2)
                dve.tensor_tensor(sv[:, :, :, 0:3:2], wv[:, :, :, 0:3:2], sums[:, :, :, 3:5], ALU.mult
                                  ).then_inc(S["sims"], 1)
                dve.tensor_tensor(sv[:, :, :, 1], wv[:, :, :, 1], sums[:, :, :, 1], ALU.mult
                                  ).then_inc(S["sims"], 1)

            def residual(b, h):
                s = b[1] % 2
                dve.wait_ge(S["conv"], at(b, 6, 3 * h + 3))
                if h == 0 and reused(b, 2):
                    dve.wait_ge(kept[s], at((b[0], b[1] // 2 * 2), 8))
                    dve.wait_ge(S["XT"], at(b, 2, -2))
                dve.tensor_tensor(x2[s][:, h * H:(h + 1) * H], CV[h][:], xs[s][:, h * H:(h + 1) * H], ALU.add
                                  ).then_inc(S["x2"], 1)

            def stats_x2(b, h):
                s = b[1] % 2
                dve.wait_ge(S["x2"], at(b, 2, 1 + h))
                dve.bn_stats(bn2[:, bass.ds(at(b), 1), h, :].rearrange("p a l -> p (a l)"),
                             x2[s][:, h * H:(h + 1) * H]).then_inc(S["bn2"], 1)

            def step(t):
                n = later(t, 1)
                if first(t):
                    logit_weights()
                if exists(t, NB):
                    for k in range(TAPS):
                        scale_x(t, 0, k)
                if exists(n, NB):
                    stats_x(n)
                if exists(t, NB):
                    for k in range(TAPS):
                        scale_x(t, 1, k)
                if exists(n, NB):
                    aggregate_x(n)
                if exists(n, NB):
                    norms(n)
                    scale_w(n)
                if exists(t, NB):
                    residual(t, 0)
                if exists(n, NB):
                    norms2(n)
                if exists(t, NB):
                    stats_x2(t, 0)
                if exists(n, NB):
                    norms3(n)
                    cosines(n)
                if exists(t, NB):
                    residual(t, 1)
                    stats_x2(t, 1)

            steps(dve, step)

            ch = [0]

            def link(ins):
                ch[0] += 1
                ins.then_inc(S["ch"], 1)
                dve.wait_ge(S["ch"], ch[0])

            def wide(a, n):
                return a.unsqueeze(2).broadcast_to([P, NB, n])

            dve.wait_ge(S["bn2"], 2 * NB)
            for b in range(NB):
                dve.bn_aggr(mv[:, b, :], bn2[:, b]).then_inc(S["mv"], 1)
            dve.wait_ge(S["mv"], NB)
            dve.wait_ge(S["raw"], NB)
            mean, var = mv[:, :, 0], mv[:, :, 1]
            dve.tensor_scalar(ve[:], var, LN_EPS, None, ALU.add).then_inc(S["v1"], 1)
            dve.wait_ge(S["a1"], 1)
            link(dve.reciprocal(rstd[:], rstd[:]))
            link(dve.tensor_tensor(rms[:], rstd[:], rstd[:], ALU.mult))
            link(dve.tensor_tensor(rms[:], rms[:], var, ALU.mult))
            link(dve.tensor_scalar(rms[:], rms[:], RMS_EPS, None, ALU.add))
            dve.sem_inc(S["v1"], 1)
            link(dve.tensor_tensor(tmp[:], wsum[:, 0:NL].unsqueeze(1).broadcast_to([P, NB, NL]),
                                   wide(mean, NL), ALU.mult))
            link(dve.tensor_tensor(tmp[:], raw[:, :, 0:NL], tmp[:], ALU.subtract))
            dve.wait_ge(S["a1"], 2)
            link(dve.reciprocal(rs[:], rs[:]))
            link(dve.tensor_tensor(rs[:], rs[:], rstd[:], ALU.mult))
            link(dve.tensor_tensor(tmp[:], tmp[:], wide(rs[:], NL), ALU.mult))
            link(dve.tensor_tensor(logit[:], tmp[:], crow[:, 0:NL].unsqueeze(1).broadcast_to([P, NB, NL]),
                                   ALU.add))
            pp = logit[:, :, 16:24].rearrange("p b (w n) -> p b w n", w=2)
            link(dve.tensor_reduce(mx[:], pp, AX.X, ALU.max))
            link(dve.tensor_tensor(hpp[:], pp, mx[:].unsqueeze(3).broadcast_to([P, NB, 2, NS]), ALU.subtract))
            link(dve.tensor_scalar(z[:].rearrange("p b i j -> p b (i j)"), logit[:, :, 0:16], 1.0 / SINKHORN_TAU,
                                   None, ALU.mult))
            link(dve.tensor_reduce(zm[:], z[:], AX.X, ALU.max))
            link(dve.tensor_tensor(z[:], z[:], zm[:].unsqueeze(3).broadcast_to([P, NB, NS, NS]), ALU.subtract))
            link(dve.tensor_reduce(zm[:], z[:].rearrange("p b i j -> p b j i"), AX.X, ALU.max))
            link(dve.tensor_tensor(z[:], z[:], zm[:].unsqueeze(2).broadcast_to([P, NB, NS, NS]), ALU.subtract))
            dve.sem_inc(S["v1"], 1)
            dve.wait_ge(S["a1"], 5)
            link(dve.tensor_reduce(hsum[:], hpp[:], AX.X, ALU.add))
            link(dve.reciprocal(hsum[:], hsum[:]))
            link(dve.tensor_tensor(hpp[:], hpp[:], hsum[:].unsqueeze(3).broadcast_to([P, NB, 2, NS]), ALU.mult))

            HB = NB // 2
            halves = [slice(0, HB), slice(HB, NB)]
            per = 6

            def iterate(i):
                shape = [P, HB, NS, NS]
                for n in range(per):
                    for hs, done in zip(halves, (S["sink0"], S["sink1"])):
                        if n or not isinstance(i, int):
                            dve.wait_ge(done, i * per + n)
                        K, W, A, B, R = kk[:, hs], kt[:, hs], av[:, hs], bv[:, hs], ssum[:, hs]
                        if n == 0:
                            ins = dve.tensor_tensor(W, K, B.unsqueeze(2).broadcast_to(shape), ALU.mult)
                        elif n == 1:
                            ins = dve.tensor_reduce(R, W, AX.X, ALU.add)
                        elif n == 2:
                            ins = dve.reciprocal(A, R)
                        elif n == 3:
                            ins = dve.tensor_tensor(W, K, A.unsqueeze(3).broadcast_to(shape), ALU.mult)
                        elif n == 4:
                            ins = dve.tensor_reduce(R, W.rearrange("p b i j -> p b j i"), AX.X, ALU.add)
                        else:
                            ins = dve.reciprocal(B, R)
                        ins.then_inc(done, 1)

            def run(start, end):
                if start == 0:
                    iterate(0)
                with dve.Fori(max(start, 1), end) as i:
                    iterate(i)
                for done in (S["sink0"], S["sink1"]):
                    dve.wait_ge(done, end * per)

            run(0, SINKHORN_ITERS // 2)
            dve.sem_inc(S["v1"], 1)
            dve.wait_ge(S["a1"], 7)
            link(dve.tensor_tensor(z[:], z[:], av[:].unsqueeze(3).broadcast_to([P, NB, NS, NS]), ALU.add))
            link(dve.tensor_tensor(z[:], z[:], ln_[:].unsqueeze(2).broadcast_to([P, NB, NS, NS]), ALU.add))
            link(dve.memset(bv[:], 1.0))
            dve.sem_inc(S["v1"], 1)
            dve.wait_ge(S["a1"], 8)
            run(SINKHORN_ITERS // 2, SINKHORN_ITERS)

            A4 = aij[:].rearrange("p b (i j) -> p b i j", i=NS)
            link(dve.tensor_tensor(kt[:], kk[:], av[:].unsqueeze(3).broadcast_to([P, NB, NS, NS]), ALU.mult))
            link(dve.tensor_tensor(A4, kt[:], bv[:].unsqueeze(2).broadcast_to([P, NB, NS, NS]), ALU.mult))
            link(dve.tensor_scalar(aij[:], aij[:], gt[:, 2:3], None, ALU.mult))
            link(dve.tensor_scalar(aij[:, :, 0:16:5], aij[:, :, 0:16:5], gt[:, 3:4], None, ALU.add))
            link(dve.tensor_scalar(rs[:], rstd[:], gt[:, 1:2], None, ALU.mult))
            link(dve.tensor_tensor(aij[:], aij[:], wide(rs[:], 16), ALU.mult))
            link(dve.tensor_reduce(zm[:], A4, AX.X, ALU.add))
            link(dve.tensor_tensor(zm[:], zm[:], wide(mean, NS), ALU.mult))
            link(dve.tensor_scalar(coefs[:, :, 24:28], zm[:], -1.0, None, ALU.mult))
            link(dve.tensor_copy(coefs[:, :, 0:16], aij[:]))
            link(dve.tensor_scalar(coefs[:, :, 0:16:5], aij[:, :, 0:16:5], 1.0, None, ALU.add))
            link(dve.tensor_scalar(coefs[:, :, 16:20], hpp[:, :, 1, :], gt[:, 1:2], None, ALU.mult))
            link(dve.tensor_tensor(coefs[:, :, 20:24], hpp[:, :, 0, :], wide(rstd[:], NS), ALU.mult))
            link(dve.tensor_reduce(pbias[:], coefs[:, :, 20:24], AX.X, ALU.add))
            link(dve.tensor_tensor(pbias[:], pbias[:], mean, ALU.mult))
            link(dve.tensor_scalar(coefs[:, :, 28], pbias[:], -1.0, None, ALU.mult))
            link(dve.memset(coefs[:, :, 29:32], 0.0))
            dve.sem_inc(S["v1"], 1)

            def pre(b):
                s = b[1] % 2
                dve.wait_ge(xmin[s], at((b[0], b[1] // 2 * 2), 8, 16))
                dve.wait_ge(S["coef"], at(b, 1, 1))
                if reused(b, 1):
                    dve.wait_ge(S["xpT"], at(b))
                for j in range(NS):
                    src = xm[s][:, j * DC:(j + 1) * DC]
                    if j == 0:
                        ins = dve.tensor_scalar(xp[:], src, coef[s][:, 20:21], coef[s][:, 28:29],
                                                ALU.mult, ALU.add)
                    else:
                        dve.wait_ge(S["pre"], at(b, NS, j))
                        ins = dve.scalar_tensor_tensor(out=xp[:], in0=src, scalar=coef[s][:, 20 + j:21 + j],
                                                       in1=xp[:], op0=ALU.mult, op1=ALU.add)
                    ins.then_inc(S["pre"], 1)

            def mix(b):
                mix_streams(dve, b, range(NS // 2), S["mixd"])

            pre((0, 0))
            pre((0, 1))
            mix((0, 0))
            with dve.Fori(1, NB // 2) as i:
                pre((i, 0))
                mix((i, -1))
                pre((i, 1))
                mix((i, 0))
            mix((0, NB - 1))

    return nc


_INS = ['x', 'ctx_4096', 'g_xattn', 'g_ffn', 'L0_xattn_weight', 'L0_ffn_W_res', 'L0_ffn_W_pre', 'L0_ffn_W_post',
        'L0_ffn_H_res_base', 'L0_ffn_H_pre_base', 'L0_ffn_H_post_base', 'L0_ffn_gate', 'L0_ffn_W_branch']
_OUTS = [((16, 128, 1024), 'float32')]


def kernel(**inputs):
    import numpy as _np
    import concourse.bacc as _bacc
    from concourse import mybir as _mybir
    from concourse.bass_utils import run_bass_kernel_spmd as _run

    nc = _bacc.Bacc("TRN2", target_bir_lowering=False, num_devices=1)
    arrays, args = {}, []
    for name in _INS:
        a = _np.ascontiguousarray(inputs[name])
        arrays[f"in_{name}_dram"] = a
        args.append(nc.dram_tensor(f"in_{name}_dram", a.shape, _mybir.dt.from_np(a.dtype), kind="ExternalInput").ap())
    for i, (shape, dtype) in enumerate(_OUTS):
        dt = _mybir.dt.from_np(_np.dtype(dtype))
        args.append(nc.dram_tensor(f"out_{i}_dram", shape, dt, kind="ExternalOutput").ap())
    build(nc, *args)
    r = _run(nc, [arrays], core_ids=[0])
    got = tuple(r.results[0][f"out_{i}_dram"] for i in range(len(_OUTS)))
    return got[0]
```

```python
from contextlib import ExitStack

import concourse.bass as bass
from concourse import mybir

F32 = mybir.dt.float32
BF16 = mybir.dt.bfloat16
ALU = mybir.AluOpType
ACT = mybir.ActivationFunctionType
AX = mybir.AxisListType

P = 128
TAPS = 3
DOTS = 2
PARTS = 3
LN_EPS = 1e-5
RMS_EPS = 1.1920929e-07
COS_EPS = 1e-8
SINKHORN_ITERS = 50
SINKHORN_TAU = 0.1


def at(b, k=1, plus=0):
    reg, off = b
    return reg * (2 * k) + (off * k + plus)


def exists(b, n):
    return not isinstance(b[0], int) or 0 <= b[1] < n


def reused(b, depth):
    return not isinstance(b[0], int) or b[1] >= depth


def ahead(eng, value):
    return value if isinstance(value, int) else eng.snap(value)


def first(b):
    return isinstance(b[0], int) and b[1] == 0


def later(b, d):
    return (b[0], b[1] + d)


def group_of(tap, c):
    return (TAPS * c + tap) // P


def build(nc, x, ctx4, g_xattn, g_ffn, weight, w_res, w_pre, w_post, res_base, pre_base, post_base, gate,
          w_branch, out):
    NB, C, T = x.shape
    NS = pre_base.shape[0]
    DC = T // NS
    NL = NS * NS + 2 * NS
    LP = 32
    NCH = T // P
    H = T // 2
    MIX = (NS + 1) * NS // 2
    MIXD = NS * NS // 2
    HB = NB // 2
    halves = (slice(0, HB), slice(HB, NB))
    HALFWAY = SINKHORN_ITERS // 2
    QW = T // 4
    assert C == P and H == 512 and NB % 2 == 0 and DC == 2 * P

    with ExitStack() as stack:
        def sb(name, shape, dt=F32):
            return stack.enter_context(nc.sbuf_tensor(name, shape, dt))

        def ps(name, shape, dt=F32):
            return stack.enter_context(nc.psum_tensor(name, shape, dt))

        def sem(name):
            return stack.enter_context(nc.semaphore(name))

        ident = sb("ident", [P, P])
        ident_b = sb("ident_b", [P, P], BF16)
        ones = sb("ones", [P, P])
        unit = sb("unit", [P, DOTS, 32])
        pick = sb("pick", [NCH * 9, NCH, 3], BF16)
        sel = sb("sel", [NCH * 9, NCH, TAPS, P], BF16)
        fold = sb("fold", [P, LP])
        w_nat = sb("w_nat", [P, C * TAPS])
        wg = sb("wg", [P, TAPS, P])
        wl_nat = sb("wl_nat", [LP, T])
        wl = sb("wl", [P, NCH, LP])
        wb = sb("wb", [P, 2, DC])
        row = sb("row", [1, LP])
        crow = sb("crow", [P, LP])
        wsum = sb("wsum", [P, LP])
        gt = sb("gt", [P, 8])
        xs = [sb(f"xs{s}", [P, T]) for s in range(2)]
        es = [sb(f"es{s}", [P, T]) for s in range(2)]
        sq = [sb(f"sq{s}", [P, T + 2]) for s in range(2)]
        pr = [sb(f"pr{s}", [P, T + 2]) for s in range(2)]
        dsb = sb("dsb", [P, QW + 2])
        nm = sb("nm", [P, NCH, 3])
        nq = sb("nq", [P, NCH, 3])
        inv = sb("inv", [P, NCH, 3])
        ww = sb("ww", [P, NCH, 3])
        sims = sb("sims", [P, NCH, 3])
        rest = sb("rest", [P, NCH, 3])
        rest2 = sb("rest2", [P, NCH, 3])
        split = sb("split", [P, NCH, 3, PARTS], BF16)
        rr = [sb(f"rr{s}", [NCH * 9, P], BF16) for s in range(2)]
        unused = sb("unused", [P, T])
        eps = sb("eps", [P, 1])
        sumx = sb("sumx", [P, 1])
        nmean = [sb(f"nmean{s}", [P, 1]) for s in range(2)]
        ssq = sb("ssq", [P, 1])
        sdx = sb("sdx", [P, 1])
        rsx = sb("rsx", [P, 1])
        ws = [sb(f"ws{s}", [P, TAPS, P]) for s in range(2)]
        gs = [sb(f"gs{k}", [P, T]) for k in range(TAPS)]
        x2 = [sb(f"x2{s}", [P, T]) for s in range(2)]
        bn2 = sb("bn2", [P, NB, 2, 6])
        xt = sb("xt", [P, NCH, P])
        lgs = sb("lgs", [P, P])
        keep = sb("keep", [P, NB, T])
        mv = sb("mv", [P, NB, 2])
        raw = sb("raw", [P, NB, LP])
        ve = sb("ve", [P, NB])
        rstd = sb("rstd", [P, NB])
        rms = sb("rms", [P, NB])
        rs = sb("rs", [P, NB])
        mx = sb("mx", [P, NB, 2])
        logit = sb("logit", [P, NB, NL])
        tmp = sb("tmp", [P, NB, NL])
        z = sb("z", [P, NB, NS, NS])
        zm = sb("zm", [P, NB, NS])
        kk = sb("kk", [P, NB, NS, NS])
        kt = sb("kt", [P, NB, NS, NS])
        ssum = sb("ssum", [P, NB, NS])
        av = sb("av", [P, NB, NS])
        bv = sb("bv", [P, NB, NS])
        ln_ = sb("ln_", [P, NB, NS])
        aij = sb("aij", [P, NB, NS * NS])
        hpp = sb("hpp", [P, NB, 2, NS])
        hsum = sb("hsum", [P, NB, 2])
        bias = sb("bias", [P, NB])
        pbias = sb("pbias", [P, NB])
        coefs = sb("coefs", [P, NB, 32])
        om = [sb(f"om{s}", [P, T]) for s in range(2)]
        dg = [sb(f"dg{s}", [P, MIX, P]) for s in range(2)]
        xp = sb("xp", [P, DC])
        xpt = sb("xpt", [P, 2, P])
        ys = [sb(f"ys{s}", [P, DC]) for s in range(2)]

        DM = ps("DM", [P, 2, 512])
        ATT = [ps(f"ATT{k}", [P, 512]) for k in range(TAPS)]
        CV = [ps(f"CV{h}", [P, 512]) for h in range(2)]
        XT = ps("XT", [P, 512])
        DT = DM[:, 0]
        RP = DM[0:NCH * 9, 1, 3 * P:3 * P + P // 2].bitcast(BF16)
        LGP = XT[:, 0:P]
        LG = XT[:, 0:LP]

        names = """wlz cdma ident unit pick sel wnat wl1 wlt wlc wgt cro crs tan tanv wgv fld padz con
            sq pr dots dsb dT nm nq inv ww sims hi res mid split RP rr att g sumx mvx ssq sdx rsx ws conv x2
            bn2 mv XT xt LGP lgs LG raw v1 a1 v2 ch
            mix pre1 pre xpT xpt y ysb seen mixd som sxp dg mixt mixo"""
        S = {n: sem("s_" + n) for n in names.split()}
        ein = [sem(f"s_ein{s}") for s in range(2)]
        xin = [sem(f"s_xin{s}") for s in range(2)]
        kept = [sem(f"s_kept{s}") for s in range(2)]
        prod = [sem(f"s_prod{e}") for e in range(2)]
        sink = [sem(f"s_sink{e}") for e in range(2)]
        outd = [sem(f"s_outd{s}") for s in range(2)]

        block = stack.enter_context(nc.Block())

        def steps(eng, step):
            for t in range(-2, 2):
                step((0, t))
            with eng.Fori(1, NB // 2 - 1) as i:
                step((i, 0))
                step((i, 1))
            for t in range(NB - 2, NB + 1):
                step((0, t))

        @block.sync
        def _(sp):
            def load_e(b):
                n = ahead(sp, at(b))
                if reused(b, 2):
                    sp.wait_ge(S["sq"], at(b, 1, -1))
                    sp.wait_ge(S["pr"], at(b, 1, -1))
                sp.dma_start(es[b[1] % 2][:], ctx4[bass.ds(n, 1)].rearrange("a c t -> (a c) t")
                             ).then_inc(ein[b[1] % 2], 16)

            def load_x(b):
                sp.dma_start(xs[b[1] % 2][:], x[bass.ds(at(b), 1)].rearrange("a c t -> (a c) t")
                             ).then_inc(xin[b[1] % 2], 16)

            def keep_x2(b):
                n = ahead(sp, at(b))
                sp.wait_ge(S["x2"], at(b, 2, 2))
                sp.dma_start(keep[:, bass.ds(n, 1), :].rearrange("p a t -> p (a t)"), x2[b[1] % 2][:]
                             ).then_inc(kept[b[1] % 2], 16)

            def step(u):
                if exists(later(u, 3), NB):
                    load_e(later(u, 3))
                keep_x2(u)
                if exists(later(u, 2), NB):
                    load_x(later(u, 2))

            load_e((0, 0))
            load_x((0, 0))
            sp.dma_start(w_nat[:], weight.rearrange("o c k -> o (c k)")).then_inc(S["wnat"], 16)
            sp.dma_start(row[:, 0:16], res_base.rearrange("(a i) j -> a (i j)", a=1)).then_inc(S["cdma"], 16)
            sp.dma_start(row[:, 16:20], pre_base.rearrange("(a i) -> a i", a=1)).then_inc(S["cdma"], 16)
            sp.dma_start(row[:, 20:24], post_base.rearrange("(a i) -> a i", a=1)).then_inc(S["cdma"], 16)
            sp.dma_start(row[:, 24:25], g_xattn.rearrange("(a i) -> a i", a=1)).then_inc(S["cdma"], 16)
            sp.dma_start(row[:, 25:26], g_ffn.rearrange("(a i) -> a i", a=1)).then_inc(S["cdma"], 16)
            sp.dma_start(row[:, 26:27], gate.rearrange("(a i) -> a i", a=1)).then_inc(S["cdma"], 16)
            load_e((0, 1))
            load_x((0, 1))
            sp.wait_ge(S["wlz"], 1)
            sp.dma_start(wl_nat[0:16, :], w_res).then_inc(S["wl1"], 16)
            sp.dma_start(wl_nat[16:20, :], w_pre).then_inc(S["wl1"], 16)
            sp.dma_start(wl_nat[20:24, :], w_post).then_inc(S["wl1"], 16)
            sp.dma_start(wb[:], w_branch.rearrange("(k c) n -> c k n", c=P)).then_inc(S["wl1"], 16)
            load_e((0, 2))
            for u in range(0, 2):
                step((0, u))
            with sp.Fori(1, NB // 2 - 2) as i:
                step((i, 0))
                step((i, 1))
            for u in range(NB - 4, NB):
                step((0, u))

            def store(b):
                n = ahead(sp, at(b))
                sp.wait_ge(S["mixd"], at(b, MIXD, MIXD))
                sp.sem_inc(S["seen"], 1)
                sp.wait_ge(S["mixo"], at(b, 2, 2))
                sp.sem_inc(S["seen"], 1)
                sp.dma_start(out[bass.ds(n, 1)].rearrange("a c t -> (a c) t"), om[b[1] % 2][:]
                             ).then_inc(outd[b[1] % 2], 16)

            with sp.Fori(0, NB // 2) as i:
                store((i, 0))
                store((i, 1))
            for s in range(2):
                sp.wait_ge(outd[s], 16 * NB // 2)

        def coef(b, c, n=1):
            return coefs[:, bass.ds(at(b), 1), c:c + n].rearrange("p a l -> p (a l)")

        def x2_of(b, j):
            return keep[:, bass.ds(at(b), 1), j * DC:(j + 1) * DC].rearrange("p a t -> p (a t)")

        @block.gpsimd
        def _(pool):
            pool.memset(wl_nat[:], 0.0).then_inc(S["wlz"], 1)
            pool.memset(ident[:], 0.0).then_inc(S["ident"], 1)
            pool.memset(ones[:], 1.0).then_inc(S["ident"], 1)
            pool.wait_ge(S["ident"], 2)
            pool.affine_select(out=ident[:], in_=ident[:], compare_op=ALU.not_equal, fill=1.0, base=0,
                               pattern=[[-1, P]], channel_multiplier=1).then_inc(S["ident"], 1)
            pool.memset(unit[:], 0.0).then_inc(S["unit"], 1)
            pool.wait_ge(S["unit"], 1)
            for m in range(DOTS):
                pool.memset(unit[:, m, m:m + 1], 1.0).then_inc(S["unit"], 1)
            pool.memset(eps[:], LN_EPS).then_inc(S["unit"], 1)
            for s in range(2):
                pool.memset(sq[s][:, 0:1], 0.0).then_inc(S["padz"], 1)
                pool.memset(sq[s][:, T + 1:T + 2], 0.0).then_inc(S["padz"], 1)
                pool.memset(pr[s][:, 0:1], 0.0).then_inc(S["padz"], 1)
                pool.memset(pr[s][:, T:T + 2], 0.0).then_inc(S["padz"], 1)
            pool.memset(gs[0][:, 0:1], 0.0).then_inc(S["padz"], 1)
            pool.memset(gs[2][:, T - 1:T], 0.0).then_inc(S["padz"], 1)
            pool.memset(pick[:], 1.0).then_inc(S["pick"], 1)
            pool.wait_ge(S["pick"], 1)
            pool.affine_select(out=pick[:], in_=pick[:], compare_op=ALU.is_ge, fill=0.0, base=0,
                               pattern=[[-9, NCH], [-3, 3]], channel_multiplier=1).then_inc(S["pick"], 1)
            pool.wait_ge(S["pick"], 2)
            pool.affine_select(out=pick[:], in_=pick[:], compare_op=ALU.is_ge, fill=0.0, base=2,
                               pattern=[[9, NCH], [3, 3]], channel_multiplier=-1).then_inc(S["pick"], 1)
            pool.memset(fold[:], 0.0).then_inc(S["fld"], 1)
            for g in range(4):
                pool.wait_ge(S["fld"], g + 1)
                pool.affine_select(out=fold[:], in_=fold[:], compare_op=ALU.not_equal, fill=1.0, base=-32 * g,
                                   pattern=[[-1, LP]], channel_multiplier=1).then_inc(S["fld"], 1)

            def products(b):
                s = b[1] % 2
                pool.wait_ge(ein[s], at((b[0], b[1] // 2 * 2), 8, 16))
                if reused(b, 2):
                    pool.wait_ge(S["dots"], at(b, 1, -1))
                pool.tensor_tensor(pr[s][:, 1:T], es[s][:, 1:T], es[s][:, 0:T - 1], ALU.mult
                                   ).then_inc(S["pr"], 1)

            one3 = ones[:, 0:3 * NCH].rearrange("p (q m) -> p q m", m=3)

            def split3(b):
                pool.wait_ge(S["sims"], at(b, 2, 2))
                if reused(b, 1):
                    pool.wait_ge(S["RP"], at(b))
                pool.tensor_tensor(split[:, :, :, 0], sims[:], one3, ALU.mult).then_inc(S["hi"], 1)
                pool.wait_ge(S["hi"], at(b, 1, 1))
                pool.tensor_tensor(rest[:], sims[:], split[:, :, :, 0], ALU.subtract).then_inc(S["res"], 1)
                pool.wait_ge(S["res"], at(b, 1, 1))
                pool.tensor_tensor(split[:, :, :, 1], rest[:], one3, ALU.mult).then_inc(S["mid"], 1)
                pool.wait_ge(S["mid"], at(b, 1, 1))
                pool.tensor_tensor(split[:, :, :, 2], rest[:], split[:, :, :, 1], ALU.subtract
                                   ).then_inc(S["split"], 1)

            def step(t):
                if exists(later(t, 2), NB):
                    products(later(t, 2))
                if exists(later(t, 1), NB):
                    split3(later(t, 1))

            steps(pool, step)

            pool.wait_ge(S["a1"], 5)

            def multiply(i):
                shape = [P, HB, NS, NS]
                for n in range(2):
                    for e, hs in enumerate(halves):
                        v = (bv, av)[n][:, hs]
                        v = v.unsqueeze(2 + n).broadcast_to(shape)
                        if n or not isinstance(i, int) or i:
                            pool.wait_ge(sink[e], i * 4 + 2 * n)
                        pool.tensor_tensor(kt[:, hs], kk[:, hs], v, ALU.mult).then_inc(prod[e], 1)

            def run(start, end, unroll):
                with pool.Fori(start, end, unroll) as i:
                    for u in range(unroll):
                        multiply(i + u)

            multiply(0)
            run(1, HALFWAY, 4)
            pool.wait_ge(S["a1"], 8)
            run(HALFWAY, SINKHORN_ITERS, 5)

            pool.wait_ge(S["v1"], 6)

            def diagonals(b):
                if reused(b, 2):
                    pool.wait_ge(S["mixt"], at(b, 1, -1))
                pool.tensor_tensor(dg[b[1] % 2][:], ident[:].unsqueeze(1).broadcast_to([P, MIX, P]),
                                   coef(b, MIX, MIX).unsqueeze(2).broadcast_to([P, MIX, P]), ALU.mult
                                   ).then_inc(S["dg"], 1)

            diagonals((0, 0))
            diagonals((0, 1))
            with pool.Fori(1, NB // 2) as i:
                diagonals((i, 0))
                diagonals((i, 1))

        @block.scalar
        def _(act):
            act.wait_ge(S["unit"], 2 + DOTS)
            act.wait_ge(S["ident"], 3)
            act.activation(ident_b[:], ident[:], ACT.Copy).then_inc(S["con"], 1)
            act.wait_ge(S["crs"], 1)
            act.activation(gt[:, 0:2], crow[:, 24:26], ACT.Tanh).then_inc(S["tan"], 1)
            act.activation(gt[:, 4:5], crow[:, 26:27], ACT.Exp, scale=-1.0).then_inc(S["tan"], 1)

            def square(b):
                s = b[1] % 2
                act.wait_ge(ein[s], at((b[0], b[1] // 2 * 2), 8, 16))
                if reused(b, 2):
                    act.wait_ge(S["dots"], at(b, 1, -1))
                act.activation(sq[s][:, 1:T + 1], es[s][:], ACT.Square).then_inc(S["sq"], 1)

            def dots_out(b):
                act.wait_ge(S["dots"], at(b, 1, 1))
                if reused(b, 1):
                    act.wait_ge(S["dT"], at(b))
                act.activation(dsb[:], DT[:, 0:QW + 2], ACT.Copy).then_inc(S["dsb"], 1)

            def mean_x(b):
                s = b[1] % 2
                act.wait_ge(xin[s], at((b[0], b[1] // 2 * 2), 8, 16))
                act.activation(unused[:], xs[s][:], ACT.Copy, accum_out=sumx[:]).then_inc(S["sumx"], 1)
                act.wait_ge(S["sumx"], at(b, 1, 1))
                act.activation(nmean[s][:], sumx[:], ACT.Copy, scale=-1.0 / T).then_inc(S["mvx"], 1)

            def deviation_x(b):
                s = b[1] % 2
                act.wait_ge(S["mvx"], at(b, 1, 1))
                act.activation(unused[:], xs[s][:], ACT.Square, bias=nmean[s][:], accum_out=ssq[:]
                               ).then_inc(S["ssq"], 1)
                act.wait_ge(S["ssq"], at(b, 1, 1))
                if reused(b, 1):
                    act.wait_ge(S["rsx"], at(b))
                act.activation(sdx[:], ssq[:], ACT.Sqrt, bias=eps[:], scale=1.0 / T).then_inc(S["sdx"], 1)

            def sqrt_sims(b):
                act.wait_ge(S["nm"], at(b, 1, 1))
                act.activation(nq[:], nm[:], ACT.Sqrt).then_inc(S["nq"], 1)

            def xt_out(b, h):
                act.wait_ge(S["XT"], at(b, 2, 1 + h))
                if h == 0 and reused(b, 1):
                    act.wait_ge(S["LGP"], at(b))
                act.activation(xt[:, 4 * h:4 * h + 4, :], XT[:].rearrange("p (a c) -> p a c", a=4), ACT.Copy
                               ).then_inc(S["xt"], 1)

            def lgp_out(b):
                act.wait_ge(S["LGP"], at(b, 1, 1))
                act.activation(lgs[:], LGP, ACT.Copy).then_inc(S["lgs"], 1)

            def rr_out(b):
                act.wait_ge(S["RP"], at(b, 1, 1))
                if reused(b, 2):
                    act.wait_ge(S["att"], at(b, 6, -6))
                act.activation(rr[b[1] % 2][:], RP, ACT.Copy).then_inc(S["rr"], 1)

            def lg_out(b):
                act.wait_ge(S["LG"], at(b, 1, 1))
                act.activation(raw[:, bass.ds(at(b), 1), :].rearrange("p a l -> p (a l)"), LG, ACT.Copy
                               ).then_inc(S["raw"], 1)

            def step(t):
                f, n, l = later(t, 2), later(t, 1), later(t, -1)
                if exists(l, NB):
                    xt_out(l, 0)
                if exists(f, NB):
                    square(f)
                if exists(n, NB):
                    dots_out(n)
                if exists(l, NB):
                    xt_out(l, 1)
                if exists(n, NB):
                    sqrt_sims(n)
                    mean_x(n)
                    deviation_x(n)
                if exists(l, NB):
                    lgp_out(l)
                if exists(n, NB):
                    rr_out(n)
                if exists(l, NB):
                    lg_out(l)

            steps(act, step)

            act.wait_ge(S["v1"], 1)
            act.activation(rstd[:], ve[:], ACT.Sqrt).then_inc(S["a1"], 1)
            act.wait_ge(S["v1"], 2)
            act.activation(rs[:], rms[:], ACT.Sqrt).then_inc(S["a1"], 1)
            act.wait_ge(S["v1"], 3)
            act.activation(hpp[:], hpp[:], ACT.Exp).then_inc(S["a1"], 1)
            act.activation(kk[:], z[:], ACT.Exp).then_inc(S["a1"], 1)
            act.activation(bv[:], zm[:], ACT.Exp).then_inc(S["a1"], 1)
            act.wait_ge(S["v1"], 4)
            act.activation(av[:], av[:], ACT.Ln).then_inc(S["a1"], 1)
            act.activation(ln_[:], bv[:], ACT.Ln).then_inc(S["a1"], 1)
            act.wait_ge(S["v1"], 5)
            act.activation(kk[:], z[:], ACT.Exp).then_inc(S["a1"], 1)

            act.wait_ge(S["v1"], 6)

            def branch_out(b):
                act.wait_ge(S["xpT"], at(b, 1, 1))
                act.activation(xpt[:], XT[:, 0:2 * P].rearrange("p (a c) -> p a c", a=2), ACT.Copy
                               ).then_inc(S["xpt"], 1)

            def y_out(b):
                act.wait_ge(S["y"], at(b, 1, 1))
                if reused(b, 2):
                    act.wait_ge(S["mixd"], at(b, MIXD, -MIXD))
                act.activation(ys[b[1] % 2][:], DT[:, 0:DC], ACT.Copy).then_inc(S["ysb"], 1)

            def start_streams(b):
                s = b[1] % 2
                if reused(b, 2):
                    act.wait_ge(outd[s], at((b[0], b[1] // 2 * 2), 8))
                for i in range(NS // 2):
                    act.activation(om[s][:, i * DC:(i + 1) * DC], x2_of(b, 0), ACT.Identity,
                                   bias=coef(b, 24 + i), scale=coef(b, 5 * i)).then_inc(S["som"], 1)

            def start_pre(b):
                if reused(b, 1):
                    act.wait_ge(S["xpT"], at(b))
                act.activation(xp[:], x2_of(b, 0), ACT.Identity, bias=coef(b, 28), scale=coef(b, 20)
                               ).then_inc(S["sxp"], 1)

            def mix_out(b):
                s = b[1] % 2
                act.wait_ge(S["mixt"], at(b, 1, 1))
                for n in range(NS // 2):
                    i = NS // 2 + n
                    act.activation(om[s][:, i * DC:(i + 1) * DC], CV[s][:, n * DC:(n + 1) * DC], ACT.Identity,
                                   bias=coef(b, 24 + i)).then_inc(S["mixo"], 1)

            def mstep(t):
                n, m = later(t, 1), later(t, 2)
                if exists(n, NB):
                    branch_out(n)
                if exists(m, NB):
                    start_pre(m)
                if exists(n, NB):
                    start_streams(n)
                    y_out(n)
                if exists(t, NB):
                    mix_out(t)

            act.wait_ge(kept[0], 16 * NB // 2)
            act.wait_ge(kept[1], 16 * NB // 2)
            start_pre((0, 0))
            for t in range(-1, 2):
                mstep((0, t))
            with act.Fori(1, NB // 2 - 1) as i:
                mstep((i, 0))
                mstep((i, 1))
            for t in range(NB - 2, NB):
                mstep((0, t))

        @block.tensor
        def _(pe):
            pe.wait_ge(S["ident"], 3)
            pe.wait_ge(S["cdma"], 6 * 16)
            pe.matmul(XT[:, 0:27], ones[0:1, :], row[0:1, 0:27], start=True, stop=True).then_inc(S["cro"], 1)
            pe.wait_ge(S["wnat"], 16)
            wv = w_nat[:].rearrange("o (c k) -> o k c", k=TAPS)
            for k in range(TAPS):
                pe.transpose(CV[0][:, k * P:(k + 1) * P], wv[:, k, :], ident[:]).then_inc(S["wgt"], 1)

            def logit_weights():
                pe.wait_ge(S["wl1"], 64)
                pe.wait_ge(S["crs"], 1)
                for j in range(NCH):
                    pe.transpose(XT[:, 64 + j * LP:64 + (j + 1) * LP], wl_nat[:, j * P:(j + 1) * P],
                                 ident[0:LP, 0:LP]).then_inc(S["wlt"], 1)
                pe.wait_ge(S["wlc"], 1)
                for j in range(NCH):
                    i = pe.matmul(XT[:, 0:LP], ones[:], wl[:, j, :], start=(j == 0), stop=(j == NCH - 1))
                i.then_inc(S["wlt"], 1)

            def dots(b):
                s = b[1] % 2
                pe.wait_ge(S["sq"], at(b, 1, 1))
                pe.wait_ge(S["pr"], at(b, 1, 1))
                if reused(b, 1):
                    pe.wait_ge(S["sims"], at(b, 2))
                for m, src in enumerate((sq, pr)):
                    for q in range(4):
                        i = pe.matmul(DT[32 * q:32 * q + 32, 0:QW + 2], unit[:, m, :],
                                      src[s][:, q * QW:(q + 1) * QW + 2], start=(m == 0),
                                      stop=(m == DOTS - 1), tile_position=(0, 32 * q))
                i.then_inc(S["dots"], 1)

            def dots_turn(b):
                pe.wait_ge(S["dsb"], at(b, 1, 1))
                if reused(b, 1):
                    pe.wait_ge(S["rr"], at(b))
                for r in range(2):
                    for d in range(3):
                        i = pe.transpose(DM[:, r, d * P:(d + 1) * P], dsb[:, r * P + d:(r + 1) * P + d], ident[:])
                i.then_inc(S["dT"], 1)

            def sims_turn(b):
                pe.wait_ge(S["split"], at(b, 1, 1))
                if reused(b, 1):
                    pe.wait_ge(S["rr"], at(b))
                pe.transpose(RP, split[:].rearrange("p a b c -> p (a b c)"), ident_b[:]).then_inc(S["RP"], 1)

            def spread(b, h, k):
                s = b[1] % 2
                if h == 0 and k == 0:
                    pe.wait_ge(S["rr"], at(b, 1, 1))
                if h or reused(b, 1):
                    pe.wait_ge(S["g"], at(b, 6, 3 * h + k + 1 - 3))
                for q in range(NCH // 2):
                    i = pe.matmul(ATT[k][:, q * P:(q + 1) * P], sel[:, 4 * h + q, k, :], rr[s][:],
                                  start=True, stop=True)
                i.then_inc(S["att"], 1)

            def conv(b, h, k):
                s = b[1] % 2
                if h == 0 and k == 0:
                    pe.wait_ge(S["ws"], at(b, 1, 1))
                if k == 0 and reused(b, 1):
                    pe.wait_ge(S["x2"], at(b, 2, h - 1))
                pe.wait_ge(S["g"], at(b, 6, 3 * h + k + 1))
                pe.matmul(CV[h][:], ws[s][:, k, :], gs[k][:, h * H:(h + 1) * H], start=(k == 0),
                          stop=(k == TAPS - 1)).then_inc(S["conv"], 1)

            def x2_turn(b, h):
                s = b[1] % 2
                pe.wait_ge(S["x2"], at(b, 2, 1 + h))
                if first(b) and h == 0:
                    pe.wait_ge(S["wlc"], 2)
                if h:
                    pe.wait_ge(S["xt"], at(b, 2, 1))
                elif reused(b, 1):
                    pe.wait_ge(S["raw"], at(b))
                for q in range(4):
                    j = 4 * h + q
                    i = pe.transpose(XT[:, q * P:(q + 1) * P], x2[s][:, j * P:(j + 1) * P], ident[:])
                i.then_inc(S["XT"], 1)

            def logits(b):
                pe.wait_ge(S["xt"], at(b, 2, 2))
                for r in range(2):
                    for g in range(4):
                        j = 4 * r + g
                        i = pe.matmul(LGP[32 * g:32 * g + 32, :], wl[:, j, :], xt[:, j, :], start=(r == 0),
                                      stop=(r == 1), tile_position=(0, 32 * g))
                i.then_inc(S["LGP"], 1)

            def logits_turn(b):
                pe.wait_ge(S["lgs"], at(b, 1, 1))
                if reused(b, 1):
                    pe.wait_ge(S["raw"], at(b))
                pe.matmul(LG, lgs[:], fold[:], start=True, stop=True).then_inc(S["LG"], 1)

            def step(t):
                n, l = later(t, 1), later(t, -1)
                if first(t):
                    logit_weights()
                if exists(t, NB):
                    for k in range(TAPS):
                        spread(t, 0, k)
                if exists(l, NB):
                    x2_turn(l, 0)
                if exists(n, NB):
                    dots(n)
                if exists(l, NB):
                    x2_turn(l, 1)
                if exists(t, NB):
                    spread(t, 1, 0)
                    conv(t, 0, 0)
                if exists(n, NB):
                    dots_turn(n)
                if exists(t, NB):
                    for k in range(1, TAPS):
                        spread(t, 1, k)
                        conv(t, 0, k)
                if exists(l, NB):
                    logits(l)
                if exists(t, NB):
                    conv(t, 1, 0)
                    conv(t, 1, 1)
                if exists(n, NB):
                    sims_turn(n)
                if exists(t, NB):
                    conv(t, 1, 2)
                if exists(l, NB):
                    logits_turn(l)

            pe.wait_ge(S["con"], 1)
            pe.wait_ge(S["unit"], 2 + DOTS)
            pe.wait_ge(S["padz"], 10)
            pe.wait_ge(S["sel"], 9)
            pe.wait_ge(S["fld"], 5)
            steps(pe, step)

            def pre_turn(b):
                pe.wait_ge(S["pre"], at(b, NS - 1, NS - 1))
                if reused(b, 1):
                    pe.wait_ge(S["xpt"], at(b))
                for r in range(2):
                    i = pe.transpose(XT[:, r * P:(r + 1) * P], xp[:, r * P:(r + 1) * P], ident[:])
                i.then_inc(S["xpT"], 1)

            def branch(b):
                pe.wait_ge(S["xpt"], at(b, 1, 1))
                if reused(b, 1):
                    pe.wait_ge(S["ysb"], at(b))
                for r in range(2):
                    i = pe.matmul(DT[:, 0:DC], xpt[:, r, :], wb[:, r, :], start=(r == 0), stop=(r == 1))
                i.then_inc(S["y"], 1)

            def mix(b, n):
                s = b[1] % 2
                if n == 0:
                    pe.wait_ge(S["dg"], at(b, 1, 1))
                    if reused(b, 2):
                        pe.wait_ge(S["mixo"], at(b, 2, -2))
                for j in range(NS + 1):
                    if n == 0 and j == NS:
                        pe.wait_ge(S["ysb"], at(b, 1, 1))
                    i = pe.matmul(CV[s][:, n * DC:(n + 1) * DC], dg[s][:, n * (NS + 1) + j, :],
                                  x2_of(b, j) if j < NS else ys[s][:], start=(j == 0), stop=(j == NS))
                if n == NS // 2 - 1:
                    i.then_inc(S["mixt"], 1)

            def mstep(t):
                n = later(t, 1)
                if exists(n, NB):
                    pre_turn(n)
                if exists(t, NB):
                    mix(t, 0)
                if exists(n, NB):
                    branch(n)
                if exists(t, NB):
                    mix(t, 1)

            for s in range(2):
                pe.wait_ge(kept[s], 16 * NB // 2)
            for t in range(-1, 2):
                mstep((0, t))
            with pe.Fori(1, NB // 2 - 1) as i:
                mstep((i, 0))
                mstep((i, 1))
            for t in range(NB - 2, NB):
                mstep((0, t))

        @block.vector
        def _(dve):
            dve.wait_ge(S["pick"], 3)
            for k in range(TAPS):
                edges = [min(c for c in range(C) if group_of(k, c) == g) for g in range(3)] + [C]
                for g in range(3):
                    n = edges[g + 1] - edges[g]
                    dve.tensor_copy(sel[:, :, k, edges[g]:edges[g + 1]],
                                    pick[:, :, g:g + 1].broadcast_to([NCH * 9, NCH, n])
                                    ).then_inc(S["sel"], 1)
            dve.wait_ge(S["cro"], 1)
            dve.tensor_copy(crow[:, 0:27], XT[:, 0:27]).then_inc(S["crs"], 1)
            dve.wait_ge(S["tan"], 2)
            dve.wait_ge(S["wgt"], 3)
            dve.tensor_scalar(wg[:].rearrange("p k o -> p (k o)"), CV[0][:, 0:TAPS * P], gt[:, 0:1], None,
                              ALU.mult).then_inc(S["wgv"], 1)
            dve.tensor_scalar(gt[:, 5:6], gt[:, 4:5], 1.0, None, ALU.add).then_inc(S["tanv"], 1)
            dve.wait_ge(S["tanv"], 1)
            dve.reciprocal(gt[:, 2:3], gt[:, 5:6]).then_inc(S["tanv"], 1)
            dve.wait_ge(S["tanv"], 2)
            dve.tensor_scalar(gt[:, 3:4], gt[:, 2:3], -1.0, 1.0, ALU.mult, ALU.add).then_inc(S["tanv"], 1)
            dve.wait_ge(S["tanv"], 3)
            dve.wait_ge(S["wgv"], 1)

            def logit_weights():
                dve.wait_ge(S["wlt"], NCH)
                dve.tensor_copy(wl[:], XT[:, 64:64 + NCH * LP].rearrange("p (j l) -> p j l", j=NCH)
                                ).then_inc(S["wlc"], 1)
                dve.wait_ge(S["wlt"], NCH + 1)
                dve.tensor_copy(wsum[:], XT[:, 0:LP]).then_inc(S["wlc"], 1)

            def scale_x(b, h, k):
                s = b[1] % 2
                lo, hi = h * H, (h + 1) * H
                t0, t1 = max(lo, 1 - k), min(hi, T + 1 - k)
                if h == 0 and k == 0:
                    dve.wait_ge(S["mvx"], at(b, 1, 1))
                dve.wait_ge(S["att"], at(b, 6, 3 * h + k + 1))
                if reused(b, 1):
                    dve.wait_ge(S["conv"], at(b, 6, 3 * h + k + 1 - 6))
                dve.scalar_tensor_tensor(out=gs[k][:, t0:t1], in0=xs[s][:, t0 + k - 1:t1 + k - 1],
                                         scalar=nmean[s][:], in1=ATT[k][:, t0 - lo:t1 - lo],
                                         op0=ALU.add, op1=ALU.mult).then_inc(S["g"], 1)

            def scale_w(b):
                s = b[1] % 2
                dve.wait_ge(S["sdx"], at(b, 1, 1))
                dve.reciprocal(rsx[:], sdx[:]).then_inc(S["rsx"], 1)
                dve.wait_ge(S["rsx"], at(b, 1, 1))
                if reused(b, 2):
                    dve.wait_ge(S["conv"], at(b, 6, -6))
                dve.tensor_scalar(ws[s][:], wg[:], rsx[:, 0:1], None, ALU.mult).then_inc(S["ws"], 1)

            sums = DM[:, :, 0:3 * P].rearrange("p r (d q m) -> p q r d m", d=3, q=4)

            def norms(b):
                dve.wait_ge(S["dT"], at(b, 1, 1))
                if reused(b, 1):
                    dve.wait_ge(S["nq"], at(b))
                dve.tensor_scalar(nm[:].rearrange("p (q r) m -> p q r m", r=2), sums[:, :, :, :, 0],
                                  COS_EPS * COS_EPS, None, ALU.max).then_inc(S["nm"], 1)

            def norms2(b):
                dve.wait_ge(S["nq"], at(b, 1, 1))
                dve.reciprocal(inv[:], nq[:]).then_inc(S["inv"], 1)

            def norms3(b):
                dve.wait_ge(S["inv"], at(b, 1, 1))
                dve.tensor_tensor(ww[:], inv[:], inv[:, :, 1:2].broadcast_to([P, NCH, 3]), ALU.mult
                                  ).then_inc(S["ww"], 1)

            def cosines(b):
                dve.wait_ge(S["ww"], at(b, 1, 1))
                if reused(b, 1):
                    dve.wait_ge(S["split"], at(b))
                wv = ww[:].rearrange("p (q r) m -> p q r m", r=2)
                sv = sims[:].rearrange("p (q r) m -> p q r m", r=2)
                dve.tensor_tensor(sv[:, :, :, 0:3:2], wv[:, :, :, 0:3:2], sums[:, :, :, 0:2, 1], ALU.mult
                                  ).then_inc(S["sims"], 1)
                dve.tensor_tensor(sv[:, :, :, 1], wv[:, :, :, 1], sums[:, :, :, 1, 0], ALU.mult
                                  ).then_inc(S["sims"], 1)

            def residual(b, h):
                s = b[1] % 2
                dve.wait_ge(S["conv"], at(b, 6, 3 * h + 3))
                if h == 0 and reused(b, 2):
                    dve.wait_ge(kept[s], at((b[0], b[1] // 2 * 2), 8))
                    dve.wait_ge(S["XT"], at(b, 2, -2))
                dve.tensor_tensor(x2[s][:, h * H:(h + 1) * H], CV[h][:], xs[s][:, h * H:(h + 1) * H], ALU.add
                                  ).then_inc(S["x2"], 1)

            def stats_x2(b, h):
                s = b[1] % 2
                dve.wait_ge(S["x2"], at(b, 2, 1 + h))
                dve.bn_stats(bn2[:, bass.ds(at(b), 1), h, :].rearrange("p a l -> p (a l)"),
                             x2[s][:, h * H:(h + 1) * H]).then_inc(S["bn2"], 1)

            def step(t):
                n, l = later(t, 1), later(t, -1)
                if first(t):
                    logit_weights()
                if exists(t, NB):
                    for k in range(TAPS):
                        scale_x(t, 0, k)
                if exists(l, NB):
                    stats_x2(l, 1)
                if exists(t, NB):
                    scale_x(t, 1, 0)
                if exists(n, NB):
                    norms(n)
                if exists(t, NB):
                    scale_x(t, 1, 1)
                if exists(n, NB):
                    norms2(n)
                    norms3(n)
                    cosines(n)
                if exists(t, NB):
                    scale_x(t, 1, 2)
                    residual(t, 0)
                if exists(n, NB):
                    scale_w(n)
                if exists(t, NB):
                    stats_x2(t, 0)
                    residual(t, 1)

            steps(dve, step)

            ch = [0]

            def link(ins):
                ch[0] += 1
                ins.then_inc(S["ch"], 1)
                dve.wait_ge(S["ch"], ch[0])

            def wide(a, n):
                return a.unsqueeze(2).broadcast_to([P, NB, n])

            dve.wait_ge(S["bn2"], 2 * NB)
            for b in range(NB):
                dve.bn_aggr(mv[:, b, :], bn2[:, b]).then_inc(S["mv"], 1)
            dve.wait_ge(S["mv"], NB)
            dve.wait_ge(S["raw"], NB)
            mean, var = mv[:, :, 0], mv[:, :, 1]
            dve.tensor_scalar(ve[:], var, LN_EPS, None, ALU.add).then_inc(S["v1"], 1)
            dve.wait_ge(S["a1"], 1)
            link(dve.reciprocal(rstd[:], rstd[:]))
            link(dve.tensor_tensor(rms[:], rstd[:], rstd[:], ALU.mult))
            link(dve.tensor_tensor(rms[:], rms[:], var, ALU.mult))
            link(dve.tensor_scalar(rms[:], rms[:], RMS_EPS, None, ALU.add))
            dve.sem_inc(S["v1"], 1)
            link(dve.tensor_tensor(tmp[:], wsum[:, 0:NL].unsqueeze(1).broadcast_to([P, NB, NL]),
                                   wide(mean, NL), ALU.mult))
            link(dve.tensor_tensor(tmp[:], raw[:, :, 0:NL], tmp[:], ALU.subtract))
            dve.wait_ge(S["a1"], 2)
            link(dve.reciprocal(rs[:], rs[:]))
            link(dve.tensor_tensor(rs[:], rs[:], rstd[:], ALU.mult))
            link(dve.tensor_tensor(tmp[:], tmp[:], wide(rs[:], NL), ALU.mult))
            link(dve.tensor_tensor(logit[:], tmp[:], crow[:, 0:NL].unsqueeze(1).broadcast_to([P, NB, NL]),
                                   ALU.add))
            pp = logit[:, :, 16:24].rearrange("p b (w n) -> p b w n", w=2)
            link(dve.tensor_reduce(mx[:], pp, AX.X, ALU.max))
            link(dve.tensor_tensor(hpp[:], pp, mx[:].unsqueeze(3).broadcast_to([P, NB, 2, NS]), ALU.subtract))
            link(dve.tensor_scalar(z[:].rearrange("p b i j -> p b (i j)"), logit[:, :, 0:16], 1.0 / SINKHORN_TAU,
                                   None, ALU.mult))
            link(dve.tensor_reduce(zm[:], z[:], AX.X, ALU.max))
            link(dve.tensor_tensor(z[:], z[:], zm[:].unsqueeze(3).broadcast_to([P, NB, NS, NS]), ALU.subtract))
            link(dve.tensor_reduce(zm[:], z[:].rearrange("p b i j -> p b j i"), AX.X, ALU.max))
            link(dve.tensor_tensor(z[:], z[:], zm[:].unsqueeze(2).broadcast_to([P, NB, NS, NS]), ALU.subtract))
            dve.sem_inc(S["v1"], 1)
            dve.wait_ge(S["a1"], 5)
            link(dve.tensor_reduce(hsum[:], hpp[:], AX.X, ALU.add))
            link(dve.reciprocal(hsum[:], hsum[:]))
            link(dve.tensor_tensor(hpp[:], hpp[:], hsum[:].unsqueeze(3).broadcast_to([P, NB, 2, NS]), ALU.mult))

            def iterate(i):
                for n in range(2):
                    for e, hs in enumerate(halves):
                        dve.wait_ge(prod[e], i * 2 + (n + 1))
                        w = kt[:, hs] if n == 0 else kt[:, hs].rearrange("p b i j -> p b j i")
                        dve.tensor_reduce(ssum[:, hs], w, AX.X, ALU.add).then_inc(sink[e], 1)
                    for e, hs in enumerate(halves):
                        dve.wait_ge(sink[e], i * 4 + (2 * n + 1))
                        dve.reciprocal((av, bv)[n][:, hs], ssum[:, hs]).then_inc(sink[e], 1)

            def run(start, end, unroll):
                with dve.Fori(start, end, unroll) as i:
                    for u in range(unroll):
                        iterate(i + u)
            iterate(0)
            run(1, HALFWAY, 4)
            for e in range(2):
                dve.wait_ge(sink[e], 4 * HALFWAY)
            dve.sem_inc(S["v1"], 1)
            dve.wait_ge(S["a1"], 7)
            link(dve.tensor_tensor(z[:], z[:], av[:].unsqueeze(3).broadcast_to([P, NB, NS, NS]), ALU.add))
            link(dve.tensor_tensor(z[:], z[:], ln_[:].unsqueeze(2).broadcast_to([P, NB, NS, NS]), ALU.add))
            link(dve.memset(bv[:], 1.0))
            dve.sem_inc(S["v1"], 1)
            dve.wait_ge(S["a1"], 8)
            run(HALFWAY, SINKHORN_ITERS, 5)
            for e in range(2):
                dve.wait_ge(sink[e], 4 * SINKHORN_ITERS)

            A4 = aij[:].rearrange("p b (i j) -> p b i j", i=NS)
            link(dve.tensor_tensor(kt[:], kk[:], av[:].unsqueeze(3).broadcast_to([P, NB, NS, NS]), ALU.mult))
            link(dve.tensor_tensor(A4, kt[:], bv[:].unsqueeze(2).broadcast_to([P, NB, NS, NS]), ALU.mult))
            link(dve.tensor_scalar(aij[:], aij[:], gt[:, 2:3], None, ALU.mult))
            link(dve.tensor_scalar(aij[:, :, 0:16:5], aij[:, :, 0:16:5], gt[:, 3:4], None, ALU.add))
            link(dve.tensor_scalar(rs[:], rstd[:], gt[:, 1:2], None, ALU.mult))
            link(dve.tensor_tensor(aij[:], aij[:], wide(rs[:], 16), ALU.mult))
            link(dve.tensor_reduce(zm[:], A4, AX.X, ALU.add))
            link(dve.tensor_tensor(zm[:], zm[:], wide(mean, NS), ALU.mult))
            c5 = coefs[:, :, 0:20].rearrange("p b (i j) -> p b i j", i=NS)
            link(dve.tensor_scalar(coefs[:, :, 24:28], zm[:], -1.0, None, ALU.mult))
            link(dve.tensor_copy(c5[:, :, :, 0:NS], A4))
            link(dve.tensor_scalar(coefs[:, :, 0:20:6], aij[:, :, 0:16:5], 1.0, None, ALU.add))
            link(dve.tensor_scalar(c5[:, :, :, NS], hpp[:, :, 1, :], gt[:, 1:2], None, ALU.mult))
            link(dve.tensor_tensor(coefs[:, :, 20:24], hpp[:, :, 0, :], wide(rstd[:], NS), ALU.mult))
            link(dve.tensor_reduce(pbias[:], coefs[:, :, 20:24], AX.X, ALU.add))
            link(dve.tensor_tensor(pbias[:], pbias[:], mean, ALU.mult))
            link(dve.tensor_scalar(coefs[:, :, 28], pbias[:], -1.0, None, ALU.mult))
            dve.sem_inc(S["v1"], 1)

            for s in range(2):
                dve.wait_ge(kept[s], 16 * NB // 2)

            def pre(b):
                for j in range(1, NS):
                    if j == 1:
                        dve.wait_ge(S["sxp"], at(b, 1, 1))
                    else:
                        dve.wait_ge(S["pre"], at(b, NS - 1, j - 1))
                    dve.scalar_tensor_tensor(out=xp[:], in0=x2_of(b, j), scalar=coef(b, 20 + j), in1=xp[:],
                                             op0=ALU.mult, op1=ALU.add).then_inc(S["pre"], 1)

            def mix(b):
                s = b[1] % 2
                for j in range(1, NS + 1):
                    for i in range(NS // 2):
                        if j == 1:
                            dve.wait_ge(S["som"], at(b, 2, i + 1))
                        else:
                            dve.wait_ge(S["mixd"], at(b, MIXD, 2 * (j - 2) + i + 1))
                        if j == NS and i == 0:
                            dve.wait_ge(S["ysb"], at(b, 1, 1))
                        o = om[s][:, i * DC:(i + 1) * DC]
                        src = x2_of(b, j) if j < NS else ys[s][:]
                        dve.scalar_tensor_tensor(out=o, in0=src, scalar=coef(b, 5 * i + j), in1=o,
                                                 op0=ALU.mult, op1=ALU.add).then_inc(S["mixd"], 1)

            pre((0, 0))
            pre((0, 1))
            mix((0, 0))
            with dve.Fori(1, NB // 2) as i:
                pre((i, 0))
                mix((i, -1))
                pre((i, 1))
                mix((i, 0))
            mix((0, NB - 1))

    return nc


_INS = ['x', 'ctx_4096', 'g_xattn', 'g_ffn', 'L0_xattn_weight', 'L0_ffn_W_res', 'L0_ffn_W_pre', 'L0_ffn_W_post',
        'L0_ffn_H_res_base', 'L0_ffn_H_pre_base', 'L0_ffn_H_post_base', 'L0_ffn_gate', 'L0_ffn_W_branch']
_OUTS = [((16, 128, 1024), 'float32')]


def kernel(**inputs):
    import numpy as _np
    import concourse.bacc as _bacc
    from concourse import mybir as _mybir
    from concourse.bass_utils import run_bass_kernel_spmd as _run

    nc = _bacc.Bacc("TRN2", target_bir_lowering=False, num_devices=1)
    arrays, args = {}, []
    for name in _INS:
        a = _np.ascontiguousarray(inputs[name])
        arrays[f"in_{name}_dram"] = a
        args.append(nc.dram_tensor(f"in_{name}_dram", a.shape, _mybir.dt.from_np(a.dtype), kind="ExternalInput").ap())
    for i, (shape, dtype) in enumerate(_OUTS):
        dt = _mybir.dt.from_np(_np.dtype(dtype))
        args.append(nc.dram_tensor(f"out_{i}_dram", shape, dt, kind="ExternalOutput").ap())
    build(nc, *args)
    r = _run(nc, [arrays], core_ids=[0])
    got = tuple(r.results[0][f"out_{i}_dram"] for i in range(len(_OUTS)))
    return got[0]
```

```python
from contextlib import ExitStack

import concourse.bass as bass
from concourse import mybir

F32 = mybir.dt.float32
BF16 = mybir.dt.bfloat16
ALU = mybir.AluOpType
ACT = mybir.ActivationFunctionType
AX = mybir.AxisListType

P = 128
TAPS = 3
DOTS = 2
PARTS = 3
LN_EPS = 1e-5
RMS_EPS = 1.1920929e-07
COS_EPS = 1e-8
SINKHORN_ITERS = 50
SINKHORN_TAU = 0.1


def at(b, k=1, plus=0):
    reg, off = b
    return reg * (2 * k) + (off * k + plus)


def exists(b, n):
    return not isinstance(b[0], int) or 0 <= b[1] < n


def reused(b, depth):
    return not isinstance(b[0], int) or b[1] >= depth


def ahead(eng, value):
    return value if isinstance(value, int) else eng.snap(value)


def first(b):
    return isinstance(b[0], int) and b[1] == 0


def later(b, d):
    return (b[0], b[1] + d)


def group_of(tap, c):
    return (TAPS * c + tap) // P


def build(nc, x, ctx4, g_xattn, g_ffn, weight, w_res, w_pre, w_post, res_base, pre_base, post_base, gate,
          w_branch, out):
    NB, C, T = x.shape
    NS = pre_base.shape[0]
    DC = T // NS
    NL = NS * NS + 2 * NS
    LP = 32
    NCH = T // P
    H = T // 2
    HS = NS // 2
    MIXT = (NS + 1) * HS
    MIXD = NS * HS + 1
    HB = NB // 2
    halves = (slice(0, HB), slice(HB, NB))
    chains = halves + (slice(HB, HB + HB // 2), slice(HB + HB // 2, NB))
    HALFWAY = SINKHORN_ITERS // 2
    PA = HALFWAY // (HB - 2)
    PM = [HALFWAY // (HB - 2)] * HB
    PM[0:2] = [PM[2] - 1, PM[2] - 1]
    PM[-2:] = [HALFWAY - sum(PM[:-2]), 0]
    FIRST = HB + 2
    QW = T // 4
    assert PA * (HB - 2) == HALFWAY - 1
    assert NS == 4 and C == P and H == 512 and NB % 2 == 0 and DC == 2 * P

    with ExitStack() as stack:
        def sb(name, shape, dt=F32):
            return stack.enter_context(nc.sbuf_tensor(name, shape, dt))

        def ps(name, shape, dt=F32):
            return stack.enter_context(nc.psum_tensor(name, shape, dt))

        def sem(name):
            return stack.enter_context(nc.semaphore(name))

        ident = sb("ident", [P, P])
        ident_b = sb("ident_b", [P, P], BF16)
        ones = sb("ones", [P, P])
        unit = sb("unit", [P, DOTS, 32])
        pick = sb("pick", [NCH * 9, NCH, 3], BF16)
        sel = sb("sel", [NCH * 9, NCH, TAPS, P], BF16)
        fold = sb("fold", [P, LP])
        w_nat = sb("w_nat", [P, C * TAPS])
        wg = sb("wg", [P, TAPS, P])
        wl_nat = sb("wl_nat", [LP, T])
        wl = sb("wl", [P, NCH, LP])
        wb = sb("wb", [P, 2, DC])
        row = sb("row", [1, LP])
        crow = sb("crow", [P, LP])
        wsum = sb("wsum", [P, LP])
        gt = sb("gt", [P, 8])
        xs = [sb(f"xs{s}", [P, T]) for s in range(2)]
        es = [sb(f"es{s}", [P, T]) for s in range(2)]
        sq = [sb(f"sq{s}", [P, T + 2]) for s in range(2)]
        pr = [sb(f"pr{s}", [P, T + 2]) for s in range(2)]
        dsb = sb("dsb", [P, QW + 2])
        nm = sb("nm", [P, NCH, 3])
        nq = sb("nq", [P, NCH, 3])
        inv = sb("inv", [P, NCH, 3])
        ww = sb("ww", [P, NCH, 3])
        sims = sb("sims", [P, NCH, 3])
        rest = sb("rest", [P, NCH, 3])
        rest2 = sb("rest2", [P, NCH, 3])
        split = sb("split", [P, NCH, 3, PARTS], BF16)
        rr = [sb(f"rr{s}", [NCH * 9, P], BF16) for s in range(2)]
        unused = sb("unused", [P, T])
        eps = sb("eps", [P, 1])
        sumx = sb("sumx", [P, 1])
        nmean = [sb(f"nmean{s}", [P, 1]) for s in range(2)]
        ssq = sb("ssq", [P, 1])
        sdx = sb("sdx", [P, 1])
        rsx = sb("rsx", [P, 1])
        ws = [sb(f"ws{s}", [P, TAPS, P]) for s in range(2)]
        gs = [sb(f"gs{k}", [P, T]) for k in range(TAPS)]
        x2 = [sb(f"x2{s}", [P, T]) for s in range(2)]
        sum2 = sb("sum2", [P, 1])
        nmean2 = sb("nmean2", [P, NB])
        ssq2 = sb("ssq2", [P, NB])
        xt = sb("xt", [P, NCH, P])
        lgs = sb("lgs", [P, P])
        keep = sb("keep", [P, NB + 2, T])
        var = sb("var", [P, NB])
        raw = sb("raw", [P, NB, LP])
        ve = sb("ve", [P, NB])
        rstd = sb("rstd", [P, NB])
        rms = sb("rms", [P, NB])
        rs = sb("rs", [P, NB])
        mx = sb("mx", [P, NB, 2])
        logit = sb("logit", [P, NB, NL])
        tmp = sb("tmp", [P, NB, NL])
        z = sb("z", [P, NB, NS, NS])
        zm = sb("zm", [P, NB, NS])
        kk = sb("kk", [P, NB, NS, NS])
        kt = sb("kt", [P, NB, NS, NS])
        ssum = sb("ssum", [P, NB, NS])
        av = sb("av", [P, NB, NS])
        bv = sb("bv", [P, NB, NS])
        ln_ = sb("ln_", [P, NB, NS])
        aij = sb("aij", [P, NB, NS * NS])
        hpp = sb("hpp", [P, NB, 2, NS])
        hsum = sb("hsum", [P, NB, 2])
        bias = sb("bias", [P, NB])
        pbias = sb("pbias", [P, NB])
        coefs = sb("coefs", [P, NB, 32])
        dg = [sb(f"dg{s}", [P, MIXT, P]) for s in range(2)]
        dpre = [sb(f"dpre{s}", [P, NS, P]) for s in range(2)]
        xp = sb("xp", [P, DC])
        xpt = sb("xpt", [P, 2, P])
        ya = sb("ya", [P, NB, DC])

        DM = ps("DM", [P, 2, 512])
        ATT = [ps(f"ATT{k}", [P, 512]) for k in range(TAPS)]
        CV = [ps(f"CV{h}", [P, 512]) for h in range(2)]
        XT = ps("XT", [P, 512])
        DT = DM[:, 0]
        RP = DM[0:NCH * 9, 1, 3 * P:3 * P + P // 2].bitcast(BF16)
        LGP = XT[:, 0:P]
        LG = XT[:, 0:LP]
        MB = [CV, ATT[0:2]]
        PB = [ATT[2], DM[:, 1]]

        names = """wlz cdma ident unit pick sel wnat wl1 wlt wlc wgt cro crs tan tanv wgv fld padz con
            sq pr dots dsb dT nm nq inv ww sims hi res mid split RP rr att g sumx mvx ssq sdx rsx ws conv x2
            sum2 nmean2 dev2 XT xt LGP lgs LG raw ch ve rstd rms rs z kk hpp lnab cmix pp
            cpre dpre xpm pre xpT xpt y ysb seen mixd som dg mixt mixo"""
        S = {n: sem("s_" + n) for n in names.split()}
        ein = [sem(f"s_ein{s}") for s in range(2)]
        xin = [sem(f"s_xin{s}") for s in range(2)]
        kept = [sem(f"s_kept{s}") for s in range(2)]
        prod = [sem(f"s_prod{e}") for e in range(4)]
        sink = [sem(f"s_sink{e}") for e in range(4)]
        outd = [sem(f"s_outd{s}") for s in range(2)]

        block = stack.enter_context(nc.Block())

        def last(t):
            return isinstance(t[0], int) and t[1] == NB

        def nothing(t, k):
            pass

        def steps(eng, step, setup=nothing, iteration=nothing):
            for t in range(-2, 2):
                step((0, t))
            with eng.Fori(1, HB // 2) as i:
                step((i, 0))
                step((i, 1))
            step((0, HB))
            step((0, HB + 1), setup)
            with eng.Fori(FIRST // 2, NB // 2 - 1) as i:
                step((i, 0), iteration)
                step((i, 1), iteration)
            step((0, NB - 2), iteration)
            step((0, NB - 1), iteration)
            step((0, NB))

        def msteps(eng, mstep):
            for t in range(0, 2):
                mstep((0, t), True)
            with eng.Fori(1, HB // 2 - 1) as i:
                mstep((i, 0), True)
                mstep((i, 1), True)
            for t in range(HB - 2, HB):
                mstep((0, t), True)
            with eng.Fori(HB // 2, NB // 2 - 1) as i:
                mstep((i, 0), False)
                mstep((i, 1), False)
            for t in range(NB - 2, NB):
                mstep((0, t), False)

        def half_a(t, k):
            final = isinstance(t[0], int) and t[1] == NB - 1
            if k >= 2 * (PA + final):
                return None
            return at(t, PA, k // 2 - PA * FIRST), k % 2

        def half_m(t, k):
            if isinstance(t[0], int):
                return (sum(PM[:t[1]]) + k // 2, k % 2) if k < 2 * PM[t[1]] else None
            return (at(t, PM[2], sum(PM[:2]) - 2 * PM[2] + k // 2), k % 2) if k < 2 * PM[2] else None

        def coef(b, c, n=1):
            return coefs[:, bass.ds(at(b), 1), c:c + n].rearrange("p a l -> p (a l)")

        def column(a, b):
            return a[:, bass.ds(at(b), 1)]

        def x2_of(b, j):
            return keep[:, bass.ds(at(b, 1, 2), 1), j * DC:(j + 1) * DC].rearrange("p a t -> p (a t)")

        def y_of(b):
            return ya[:, bass.ds(at(b), 1), :].rearrange("p a c -> p (a c)")

        def out_of(b, i, n=1):
            return keep[:, bass.ds(at(b), 1), i * DC:(i + n) * DC].rearrange("p a t -> p (a t)")

        @block.sync
        def _(sp):
            def load_e(b):
                n = ahead(sp, at(b))
                if reused(b, 2):
                    sp.wait_ge(S["sq"], at(b, 1, -1))
                    sp.wait_ge(S["pr"], at(b, 1, -1))
                sp.dma_start(es[b[1] % 2][:], ctx4[bass.ds(n, 1)].rearrange("a c t -> (a c) t")
                             ).then_inc(ein[b[1] % 2], 16)

            def load_x(b):
                sp.dma_start(xs[b[1] % 2][:], x[bass.ds(at(b), 1)].rearrange("a c t -> (a c) t")
                             ).then_inc(xin[b[1] % 2], 16)

            def keep_x2(b):
                n = ahead(sp, at(b))
                sp.wait_ge(S["x2"], at(b, 2, 2))
                sp.dma_start(keep[:, bass.ds(n + 2, 1), :].rearrange("p a t -> p (a t)"), x2[b[1] % 2][:]
                             ).then_inc(kept[b[1] % 2], 16)

            def step(u):
                if exists(later(u, 3), NB):
                    load_e(later(u, 3))
                keep_x2(u)
                if exists(later(u, 2), NB):
                    load_x(later(u, 2))

            load_e((0, 0))
            load_x((0, 0))
            sp.dma_start(w_nat[:], weight.rearrange("o c k -> o (c k)")).then_inc(S["wnat"], 16)
            sp.dma_start(row[:, 0:16], res_base.rearrange("(a i) j -> a (i j)", a=1)).then_inc(S["cdma"], 16)
            sp.dma_start(row[:, 16:20], pre_base.rearrange("(a i) -> a i", a=1)).then_inc(S["cdma"], 16)
            sp.dma_start(row[:, 20:24], post_base.rearrange("(a i) -> a i", a=1)).then_inc(S["cdma"], 16)
            sp.dma_start(row[:, 24:25], g_xattn.rearrange("(a i) -> a i", a=1)).then_inc(S["cdma"], 16)
            sp.dma_start(row[:, 25:26], g_ffn.rearrange("(a i) -> a i", a=1)).then_inc(S["cdma"], 16)
            sp.dma_start(row[:, 26:27], gate.rearrange("(a i) -> a i", a=1)).then_inc(S["cdma"], 16)
            load_e((0, 1))
            load_x((0, 1))
            sp.wait_ge(S["wlz"], 1)
            sp.dma_start(wl_nat[0:16, :], w_res).then_inc(S["wl1"], 16)
            sp.dma_start(wl_nat[16:20, :], w_pre).then_inc(S["wl1"], 16)
            sp.dma_start(wl_nat[20:24, :], w_post).then_inc(S["wl1"], 16)
            sp.dma_start(wb[:], w_branch.rearrange("(k c) n -> c k n", c=P)).then_inc(S["wl1"], 16)
            load_e((0, 2))
            for u in range(0, 2):
                step((0, u))
            with sp.Fori(1, NB // 2 - 2) as i:
                step((i, 0))
                step((i, 1))
            for u in range(NB - 4, NB):
                step((0, u))

            def store(b):
                n = ahead(sp, at(b))
                sp.wait_ge(S["mixd"], at(b, MIXD, MIXD))
                sp.sem_inc(S["seen"], 1)
                sp.wait_ge(S["mixo"], at(b, HS, HS))
                sp.sem_inc(S["seen"], 1)
                sp.dma_start(out[bass.ds(n, 1)].rearrange("a c t -> (a c) t"), out_of(b, 0, NS)
                             ).then_inc(outd[b[1] % 2], 16)

            with sp.Fori(0, NB // 2) as i:
                store((i, 0))
                store((i, 1))
            for s in range(2):
                sp.wait_ge(outd[s], 16 * NB // 2)

        @block.gpsimd
        def _(pool):
            pool.memset(wl_nat[:], 0.0).then_inc(S["wlz"], 1)
            pool.memset(ident[:], 0.0).then_inc(S["ident"], 1)
            pool.memset(ones[:], 1.0).then_inc(S["ident"], 1)
            pool.wait_ge(S["ident"], 2)
            pool.affine_select(out=ident[:], in_=ident[:], compare_op=ALU.not_equal, fill=1.0, base=0,
                               pattern=[[-1, P]], channel_multiplier=1).then_inc(S["ident"], 1)
            pool.memset(unit[:], 0.0).then_inc(S["unit"], 1)
            pool.wait_ge(S["unit"], 1)
            for m in range(DOTS):
                pool.memset(unit[:, m, m:m + 1], 1.0).then_inc(S["unit"], 1)
            pool.memset(eps[:], LN_EPS).then_inc(S["unit"], 1)
            for s in range(2):
                pool.memset(sq[s][:, 0:1], 0.0).then_inc(S["padz"], 1)
                pool.memset(sq[s][:, T + 1:T + 2], 0.0).then_inc(S["padz"], 1)
                pool.memset(pr[s][:, 0:1], 0.0).then_inc(S["padz"], 1)
                pool.memset(pr[s][:, T:T + 2], 0.0).then_inc(S["padz"], 1)
            pool.memset(gs[0][:, 0:1], 0.0).then_inc(S["padz"], 1)
            pool.memset(gs[2][:, T - 1:T], 0.0).then_inc(S["padz"], 1)
            pool.memset(pick[:], 1.0).then_inc(S["pick"], 1)
            pool.wait_ge(S["pick"], 1)
            pool.affine_select(out=pick[:], in_=pick[:], compare_op=ALU.is_ge, fill=0.0, base=0,
                               pattern=[[-9, NCH], [-3, 3]], channel_multiplier=1).then_inc(S["pick"], 1)
            pool.wait_ge(S["pick"], 2)
            pool.affine_select(out=pick[:], in_=pick[:], compare_op=ALU.is_ge, fill=0.0, base=2,
                               pattern=[[9, NCH], [3, 3]], channel_multiplier=-1).then_inc(S["pick"], 1)
            pool.memset(fold[:], 0.0).then_inc(S["fld"], 1)
            for g in range(4):
                pool.wait_ge(S["fld"], g + 1)
                pool.affine_select(out=fold[:], in_=fold[:], compare_op=ALU.not_equal, fill=1.0, base=-32 * g,
                                   pattern=[[-1, LP]], channel_multiplier=1).then_inc(S["fld"], 1)

            def products(b, q):
                s = b[1] % 2
                if q == 0:
                    pool.wait_ge(ein[s], at((b[0], b[1] // 2 * 2), 8, 16))
                    if reused(b, 2):
                        pool.wait_ge(S["dots"], at(b, 1, -1))
                lo, hi = max(q * QW, 1), (q + 1) * QW
                i = pool.tensor_tensor(pr[s][:, lo:hi], es[s][:, lo:hi], es[s][:, lo - 1:hi - 1], ALU.mult)
                if q == 3:
                    i.then_inc(S["pr"], 1)

            one3 = ones[:, 0:3 * NCH].rearrange("p (q m) -> p q m", m=3)

            def split3(b):
                pool.wait_ge(S["sims"], at(b, 2, 2))
                if reused(b, 1):
                    pool.wait_ge(S["RP"], at(b))
                pool.tensor_tensor(split[:, :, :, 0], sims[:], one3, ALU.mult).then_inc(S["hi"], 1)
                pool.wait_ge(S["hi"], at(b, 1, 1))
                pool.tensor_tensor(rest[:], sims[:], split[:, :, :, 0], ALU.subtract).then_inc(S["res"], 1)
                pool.wait_ge(S["res"], at(b, 1, 1))
                pool.tensor_tensor(split[:, :, :, 1], rest[:], one3, ALU.mult).then_inc(S["mid"], 1)
                pool.wait_ge(S["mid"], at(b, 1, 1))
                pool.tensor_tensor(split[:, :, :, 2], rest[:], split[:, :, :, 1], ALU.subtract
                                   ).then_inc(S["split"], 1)

            def multiply(i, n, e):
                hs = chains[e]
                v = (bv, av)[n][:, hs]
                pool.wait_ge(sink[e], i * 4 + (2 * n + 1))
                shape = [P, hs.stop - hs.start, NS, NS]
                pool.tensor_tensor(kt[:, hs], kk[:, hs], v.unsqueeze(2 + n).broadcast_to(shape), ALU.mult
                                   ).then_inc(prod[e], 1)

            def multiply_a(t, k):
                h = half_a(t, k)
                if h:
                    multiply(*h, 0)

            def step(t, beside=nothing):
                for q in range(4):
                    beside(t, q)
                    if exists(later(t, 2), NB):
                        products(later(t, 2), q)
                beside(t, 4)
                if exists(later(t, 1), NB):
                    split3(later(t, 1))
                for k in range(5, 10):
                    beside(t, k)

            steps(pool, step, nothing, multiply_a)

            pool.wait_ge(S["kk"], 3)
            with pool.Fori(0, HALFWAY, 5) as i:
                for u in range(5):
                    for n in range(2):
                        multiply(i + (HALFWAY + u), n, 0)
                        multiply(i + u, n, 1)

            pool.wait_ge(S["cmix"], 1)

            def diagonals(b, c, early):
                count = MIXT if early else MIXT - 1
                lo, hi = 2 * c, min(2 * c + 2, count)
                if c == 0 and reused(b, 2):
                    pool.wait_ge(S["mixt"], at(b, HS, -HS))
                i = pool.tensor_tensor(dg[b[1] % 2][:, lo:hi], ident[:].unsqueeze(1).broadcast_to([P, hi - lo, P]),
                                       coef(b, HS * (NS + 1) + lo, hi - lo).unsqueeze(2).broadcast_to([P, hi - lo, P]),
                                       ALU.mult)
                if hi == count:
                    i.then_inc(S["dg"], 1)

            def mstep(t):
                n = later(t, 1)
                for k in range(10):
                    if half_m(t, k):
                        for e in (2, 3):
                            multiply(*half_m(t, k), e)
                    if k < 5 and exists(n, HB):
                        diagonals(n, k, True)

            for c in range(5):
                diagonals((0, 0), c, True)
            for t in range(0, 2):
                mstep((0, t))
            with pool.Fori(1, HB // 2 - 1) as i:
                mstep((i, 0))
                mstep((i, 1))
            for t in range(HB - 2, HB):
                mstep((0, t))
            pool.wait_ge(S["cmix"], 2)
            with pool.Fori(HB // 2, NB // 2) as i:
                for c in range(5):
                    diagonals((i, 0), c, False)
                for c in range(5):
                    diagonals((i, 1), c, False)

        @block.scalar
        def _(act):
            act.wait_ge(S["unit"], 2 + DOTS)
            act.wait_ge(S["ident"], 3)
            act.activation(ident_b[:], ident[:], ACT.Copy).then_inc(S["con"], 1)
            act.wait_ge(S["crs"], 1)
            act.activation(gt[:, 0:2], crow[:, 24:26], ACT.Tanh).then_inc(S["tan"], 1)
            act.activation(gt[:, 4:5], crow[:, 26:27], ACT.Exp, scale=-1.0).then_inc(S["tan"], 1)

            def square(b):
                s = b[1] % 2
                act.wait_ge(ein[s], at((b[0], b[1] // 2 * 2), 8, 16))
                if reused(b, 2):
                    act.wait_ge(S["dots"], at(b, 1, -1))
                act.activation(sq[s][:, 1:T + 1], es[s][:], ACT.Square).then_inc(S["sq"], 1)

            def dots_out(b):
                act.wait_ge(S["dots"], at(b, 1, 1))
                if reused(b, 1):
                    act.wait_ge(S["dT"], at(b))
                act.activation(dsb[:], DT[:, 0:QW + 2], ACT.Copy).then_inc(S["dsb"], 1)

            def mean_x(b):
                s = b[1] % 2
                act.wait_ge(xin[s], at((b[0], b[1] // 2 * 2), 8, 16))
                act.activation(unused[:], xs[s][:], ACT.Copy, accum_out=sumx[:]).then_inc(S["sumx"], 1)
                act.wait_ge(S["sumx"], at(b, 1, 1))
                act.activation(nmean[s][:], sumx[:], ACT.Copy, scale=-1.0 / T).then_inc(S["mvx"], 1)

            def deviation_x(b):
                s = b[1] % 2
                act.wait_ge(S["mvx"], at(b, 1, 1))
                act.activation(unused[:], xs[s][:], ACT.Square, bias=nmean[s][:], accum_out=ssq[:]
                               ).then_inc(S["ssq"], 1)
                act.wait_ge(S["ssq"], at(b, 1, 1))
                if reused(b, 1):
                    act.wait_ge(S["rsx"], at(b))
                act.activation(sdx[:], ssq[:], ACT.Sqrt, bias=eps[:], scale=1.0 / T).then_inc(S["sdx"], 1)

            def sqrt_sims(b):
                act.wait_ge(S["nm"], at(b, 1, 1))
                act.activation(nq[:], nm[:], ACT.Sqrt).then_inc(S["nq"], 1)

            def scale_w(b):
                s = b[1] % 2
                act.wait_ge(S["rsx"], at(b, 1, 1))
                if reused(b, 2):
                    act.wait_ge(S["conv"], at(b, 6, -6))
                act.activation(ws[s][:], wg[:], ACT.Copy, scale=rsx[:]).then_inc(S["ws"], 1)

            def mean_x2(b):
                act.wait_ge(S["x2"], at(b, 2, 2))
                act.activation(unused[:], x2[b[1] % 2][:], ACT.Copy, accum_out=sum2[:]).then_inc(S["sum2"], 1)
                act.wait_ge(S["sum2"], at(b, 1, 1))
                act.activation(column(nmean2, b), sum2[:], ACT.Copy, scale=-1.0 / T).then_inc(S["nmean2"], 1)

            def deviation_x2(b):
                act.wait_ge(S["nmean2"], at(b, 1, 1))
                act.activation(unused[:], x2[b[1] % 2][:], ACT.Square, bias=column(nmean2, b),
                               accum_out=column(ssq2, b)).then_inc(S["dev2"], 1)

            def xt_out(b, h):
                act.wait_ge(S["XT"], at(b, 2, 1 + h))
                if h == 0 and reused(b, 1):
                    act.wait_ge(S["LGP"], at(b))
                act.activation(xt[:, 4 * h:4 * h + 4, :], XT[:].rearrange("p (a c) -> p a c", a=4), ACT.Copy
                               ).then_inc(S["xt"], 1)

            def lgp_out(b):
                act.wait_ge(S["LGP"], at(b, 1, 1))
                act.activation(lgs[:], LGP, ACT.Copy).then_inc(S["lgs"], 1)

            def rr_out(b):
                act.wait_ge(S["RP"], at(b, 1, 1))
                if reused(b, 2):
                    act.wait_ge(S["att"], at(b, 6, -6))
                act.activation(rr[b[1] % 2][:], RP, ACT.Copy).then_inc(S["rr"], 1)

            def lg_out(b):
                act.wait_ge(S["LG"], at(b, 1, 1))
                act.activation(raw[:, bass.ds(at(b), 1), :].rearrange("p a l -> p (a l)"), LG, ACT.Copy
                               ).then_inc(S["raw"], 1)

            def setup(t, k):
                sinkhorn_start(0, k)

            def sinkhorn_start(e, k):
                hs = halves[e]
                if k == 0:
                    act.wait_ge(S["ve"], e + 1)
                    act.activation(rstd[:, hs], ve[:, hs], ACT.Sqrt).then_inc(S["rstd"], 1)
                if k == 1:
                    act.wait_ge(S["rms"], e + 1)
                    act.activation(rs[:, hs], rms[:, hs], ACT.Sqrt).then_inc(S["rs"], 1)
                if k == 2:
                    act.wait_ge(S["z"], e + 1)
                    act.activation(kk[:, hs], z[:, hs], ACT.Exp).then_inc(S["kk"], 1)
                    act.activation(bv[:, hs], zm[:, hs], ACT.Exp).then_inc(sink[e], 1)
                if k == 2 and e == 0:
                    act.activation(gt[:, 7:8], eps[:], ACT.Sqrt)

            def step(t, beside=nothing):
                f, n, l = later(t, 2), later(t, 1), later(t, -1)
                if exists(l, NB):
                    xt_out(l, 0)
                if exists(f, NB):
                    square(f)
                if first(n):
                    act.activation(gt[:, 7:8], eps[:], ACT.Sqrt)
                beside(t, 0)
                if exists(n, NB):
                    dots_out(n)
                if exists(l, NB):
                    xt_out(l, 1)
                    mean_x2(l)
                beside(t, 1)
                if exists(n, NB):
                    sqrt_sims(n)
                    mean_x(n)
                    deviation_x(n)
                if exists(l, NB):
                    lgp_out(l)
                    deviation_x2(l)
                if last(t):
                    sinkhorn_start(1, 0)
                if exists(n, NB):
                    rr_out(n)
                    scale_w(n)
                if last(t):
                    sinkhorn_start(1, 1)
                if exists(l, NB):
                    lg_out(l)
                beside(t, 2)

            steps(act, step, setup)

            def logarithms(e, its):
                act.wait_ge(sink[e], 1 + 4 * its)
                act.activation(ln_[:, halves[e]], bv[:, halves[e]], ACT.Ln).then_inc(S["lnab"], 1)
                act.activation(av[:, halves[e]], av[:, halves[e]], ACT.Ln).then_inc(S["lnab"], 1)

            logarithms(0, HALFWAY)
            sinkhorn_start(1, 2)
            act.wait_ge(S["z"], 3)
            act.activation(kk[:, halves[0]], z[:, halves[0]], ACT.Exp).then_inc(S["kk"], 1)
            act.wait_ge(S["pp"], 1)
            act.activation(hpp[:], hpp[:], ACT.Exp).then_inc(S["hpp"], 1)

            def pre_diagonals(b):
                if reused(b, 2):
                    act.wait_ge(S["xpm"], at(b, 1, -1))
                for j in range(NS):
                    act.activation(dpre[b[1] % 2][:, j, :], ident[:], ACT.Copy, scale=coef(b, 20 + j)
                                   ).then_inc(S["dpre"], 1)

            def pre_out(b):
                act.wait_ge(S["xpm"], at(b, 1, 1))
                if reused(b, 1):
                    act.wait_ge(S["xpT"], at(b))
                act.activation(xp[:], PB[b[1] % 2][:, 0:DC], ACT.Identity, bias=coef(b, 28)
                               ).then_inc(S["pre"], 1)

            def branch_out(b):
                act.wait_ge(S["xpT"], at(b, 1, 1))
                act.activation(xpt[:], XT[:, 0:2 * P].rearrange("p (a c) -> p a c", a=2), ACT.Copy
                               ).then_inc(S["xpt"], 1)

            def y_out(b):
                act.wait_ge(S["y"], at(b, 1, 1))
                act.activation(y_of(b), DT[:, 0:DC], ACT.Copy).then_inc(S["ysb"], 1)

            def ystep(b):
                pre_out(b)
                branch_out(b)
                if exists(later(b, 2), NB):
                    pre_diagonals(later(b, 2))
                y_out(b)

            act.wait_ge(S["cpre"], 1)
            pre_diagonals((0, 0))
            pre_diagonals((0, 1))
            ystep((0, 0))
            ystep((0, 1))
            with act.Fori(1, HB // 2) as i:
                ystep((i, 0))
                ystep((i, 1))

            def start_streams(b):
                if reused(b, 2):
                    act.wait_ge(S["mixd"], at(b, MIXD, -MIXD))
                    act.wait_ge(S["mixt"], at(b, HS, -HS))
                for i in range(HS):
                    act.activation(out_of(b, i), x2_of(b, 0), ACT.Identity, bias=coef(b, 24 + i),
                                   scale=coef(b, (NS + 1) * i)).then_inc(S["som"], 1)

            def mix_out(b, n):
                act.wait_ge(S["mixt"], at(b, HS, HS - n))
                act.activation(out_of(b, HS + n), MB[n][b[1] % 2][:, 0:DC], ACT.Identity,
                               bias=coef(b, 24 + HS + n)).then_inc(S["mixo"], 1)

            def mstep(t, early):
                if early:
                    pre_out(later(t, HB))
                mix_out(t, 1)
                if early and t[1] == HB - 1:
                    act.wait_ge(S["cmix"], 2)
                if exists(later(t, 1), NB):
                    start_streams(later(t, 1))
                if early:
                    branch_out(later(t, HB))
                mix_out(t, 0)
                if early:
                    if exists(later(t, HB + 2), NB):
                        pre_diagonals(later(t, HB + 2))
                    y_out(later(t, HB))

            logarithms(1, HALFWAY)
            act.wait_ge(kept[0], 16 * NB // 2)
            act.wait_ge(kept[1], 16 * NB // 2)
            act.wait_ge(S["z"], 4)
            for e in (2, 3):
                act.activation(kk[:, chains[e]], z[:, chains[e]], ACT.Exp).then_inc(sink[e], 1)
            act.wait_ge(S["cmix"], 1)
            start_streams((0, 0))
            msteps(act, mstep)

        @block.tensor
        def _(pe):
            pe.wait_ge(S["ident"], 3)
            pe.wait_ge(S["cdma"], 6 * 16)
            pe.matmul(XT[:, 0:27], ones[0:1, :], row[0:1, 0:27], start=True, stop=True).then_inc(S["cro"], 1)
            pe.wait_ge(S["wnat"], 16)
            wv = w_nat[:].rearrange("o (c k) -> o k c", k=TAPS)
            for k in range(TAPS):
                pe.transpose(CV[0][:, k * P:(k + 1) * P], wv[:, k, :], ident[:]).then_inc(S["wgt"], 1)

            def logit_weights():
                pe.wait_ge(S["wl1"], 64)
                pe.wait_ge(S["crs"], 1)
                for j in range(NCH):
                    pe.transpose(XT[:, 64 + j * LP:64 + (j + 1) * LP], wl_nat[:, j * P:(j + 1) * P],
                                 ident[0:LP, 0:LP]).then_inc(S["wlt"], 1)

            def logit_weight_sums():
                pe.wait_ge(S["wlc"], 1)
                for j in range(NCH):
                    i = pe.matmul(XT[:, 0:LP], ones[:], wl[:, j, :], start=(j == 0), stop=(j == NCH - 1))
                i.then_inc(S["wlt"], 1)

            def dots(b):
                s = b[1] % 2
                pe.wait_ge(S["sq"], at(b, 1, 1))
                pe.wait_ge(S["pr"], at(b, 1, 1))
                if reused(b, 1):
                    pe.wait_ge(S["sims"], at(b, 2))
                for m, src in enumerate((sq, pr)):
                    for q in range(4):
                        i = pe.matmul(DT[32 * q:32 * q + 32, 0:QW + 2], unit[:, m, :],
                                      src[s][:, q * QW:(q + 1) * QW + 2], start=(m == 0),
                                      stop=(m == DOTS - 1), tile_position=(0, 32 * q))
                i.then_inc(S["dots"], 1)

            def dots_turn(b):
                pe.wait_ge(S["dsb"], at(b, 1, 1))
                if reused(b, 1):
                    pe.wait_ge(S["rr"], at(b))
                for r in range(2):
                    for d in range(3):
                        i = pe.transpose(DM[:, r, d * P:(d + 1) * P], dsb[:, r * P + d:(r + 1) * P + d], ident[:])
                i.then_inc(S["dT"], 1)

            def sims_turn(b):
                pe.wait_ge(S["split"], at(b, 1, 1))
                if reused(b, 1):
                    pe.wait_ge(S["rr"], at(b))
                pe.transpose(RP, split[:].rearrange("p a b c -> p (a b c)"), ident_b[:]).then_inc(S["RP"], 1)

            def spread(b, h, k):
                s = b[1] % 2
                if h == 0 and k == 0:
                    pe.wait_ge(S["rr"], at(b, 1, 1))
                if h or reused(b, 1):
                    pe.wait_ge(S["g"], at(b, 6, 3 * h + k + 1 - 3))
                for q in range(NCH // 2):
                    i = pe.matmul(ATT[k][:, q * P:(q + 1) * P], sel[:, 4 * h + q, k, :], rr[s][:],
                                  start=True, stop=True)
                i.then_inc(S["att"], 1)

            def conv(b, h, k):
                s = b[1] % 2
                if h == 0 and k == 0:
                    pe.wait_ge(S["ws"], at(b, 1, 1))
                if k == 0 and reused(b, 1):
                    pe.wait_ge(S["x2"], at(b, 2, h - 1))
                pe.wait_ge(S["g"], at(b, 6, 3 * h + k + 1))
                pe.matmul(CV[h][:], ws[s][:, k, :], gs[k][:, h * H:(h + 1) * H], start=(k == 0),
                          stop=(k == TAPS - 1)).then_inc(S["conv"], 1)

            def x2_turn(b, h):
                s = b[1] % 2
                pe.wait_ge(S["x2"], at(b, 2, 1 + h))
                if first(b) and h == 0:
                    pe.wait_ge(S["wlc"], 2)
                if h:
                    pe.wait_ge(S["xt"], at(b, 2, 1))
                elif reused(b, 1):
                    pe.wait_ge(S["raw"], at(b))
                for q in range(4):
                    j = 4 * h + q
                    i = pe.transpose(XT[:, q * P:(q + 1) * P], x2[s][:, j * P:(j + 1) * P], ident[:])
                i.then_inc(S["XT"], 1)

            def logits(b):
                pe.wait_ge(S["xt"], at(b, 2, 2))
                for r in range(2):
                    for g in range(4):
                        j = 4 * r + g
                        i = pe.matmul(LGP[32 * g:32 * g + 32, :], wl[:, j, :], xt[:, j, :], start=(r == 0),
                                      stop=(r == 1), tile_position=(0, 32 * g))
                i.then_inc(S["LGP"], 1)

            def logits_turn(b):
                pe.wait_ge(S["lgs"], at(b, 1, 1))
                if reused(b, 1):
                    pe.wait_ge(S["raw"], at(b))
                pe.matmul(LG, lgs[:], fold[:], start=True, stop=True).then_inc(S["LG"], 1)

            def step(t, beside=nothing):
                n, l = later(t, 1), later(t, -1)
                if exists(t, NB):
                    for k in range(TAPS):
                        spread(t, 0, k)
                if exists(l, NB):
                    x2_turn(l, 0)
                if exists(n, NB):
                    dots(n)
                if exists(l, NB):
                    x2_turn(l, 1)
                if exists(t, NB):
                    spread(t, 1, 0)
                    conv(t, 0, 0)
                if exists(n, NB):
                    dots_turn(n)
                if exists(t, NB):
                    for k in range(1, TAPS):
                        spread(t, 1, k)
                        conv(t, 0, k)
                if exists(l, NB):
                    logits(l)
                if first(t):
                    logit_weights()
                if exists(t, NB):
                    conv(t, 1, 0)
                    conv(t, 1, 1)
                if exists(n, NB):
                    sims_turn(n)
                if exists(t, NB):
                    conv(t, 1, 2)
                if first(t):
                    logit_weight_sums()
                if exists(l, NB):
                    logits_turn(l)

            pe.wait_ge(S["con"], 1)
            pe.wait_ge(S["unit"], 2 + DOTS)
            pe.wait_ge(S["padz"], 10)
            pe.wait_ge(S["sel"], 9)
            pe.wait_ge(S["fld"], 5)
            steps(pe, step)

            def pre(b):
                s = b[1] % 2
                pe.wait_ge(S["dpre"], at(b, NS, NS))
                if reused(b, 2):
                    pe.wait_ge(S["pre"], at(b, 1, -1))
                for j in range(NS):
                    i = pe.matmul(PB[s][:, 0:DC], dpre[s][:, j, :], x2_of(b, j), start=(j == 0),
                                  stop=(j == NS - 1))
                i.then_inc(S["xpm"], 1)

            def pre_turn(b):
                pe.wait_ge(S["pre"], at(b, 1, 1))
                if reused(b, 1):
                    pe.wait_ge(S["xpt"], at(b))
                for r in range(2):
                    i = pe.transpose(XT[:, r * P:(r + 1) * P], xp[:, r * P:(r + 1) * P], ident[:])
                i.then_inc(S["xpT"], 1)

            def branch(b):
                pe.wait_ge(S["xpt"], at(b, 1, 1))
                if reused(b, 1):
                    pe.wait_ge(S["ysb"], at(b))
                for r in range(2):
                    i = pe.matmul(DT[:, 0:DC], xpt[:, r, :], wb[:, r, :], start=(r == 0), stop=(r == 1))
                i.then_inc(S["y"], 1)

            def ystep(b):
                pre_turn(b)
                if exists(later(b, 1), NB):
                    pre(later(b, 1))
                branch(b)

            for s in range(2):
                pe.wait_ge(kept[s], 16 * NB // 2)
            pre((0, 0))
            ystep((0, 0))
            ystep((0, 1))
            with pe.Fori(1, HB // 2) as i:
                ystep((i, 0))
                ystep((i, 1))

            def mix(b, n, early):
                s = b[1] % 2
                if n == 1:
                    pe.wait_ge(S["dg"], at(b, 1, 1))
                if reused(b, 2):
                    pe.wait_ge(S["mixo"], at(b, HS, -HS - n))
                last = NS if early or n == 0 else NS - 1
                for j in range(last + 1):
                    if j == NS:
                        pe.wait_ge(S["ysb"], at(b, 1, 1))
                    i = pe.matmul(MB[n][s][:, 0:DC], dg[s][:, n * (NS + 1) + j, :],
                                  x2_of(b, j) if j < NS else y_of(b), start=(j == 0), stop=(j == last))
                i.then_inc(S["mixt"], 1)

            def mstep(t, early):
                mix(t, 1, early)
                if early:
                    pre_turn(later(t, HB))
                mix(t, 0, early)
                if early:
                    if exists(later(t, HB + 1), NB):
                        pre(later(t, HB + 1))
                    branch(later(t, HB))

            msteps(pe, mstep)

        @block.vector
        def _(dve):
            dve.wait_ge(S["pick"], 3)
            for k in range(TAPS):
                edges = [min(c for c in range(C) if group_of(k, c) == g) for g in range(3)] + [C]
                for g in range(3):
                    n = edges[g + 1] - edges[g]
                    dve.tensor_copy(sel[:, :, k, edges[g]:edges[g + 1]],
                                    pick[:, :, g:g + 1].broadcast_to([NCH * 9, NCH, n])
                                    ).then_inc(S["sel"], 1)
            dve.wait_ge(S["cro"], 1)
            dve.tensor_copy(crow[:, 0:27], XT[:, 0:27]).then_inc(S["crs"], 1)
            dve.wait_ge(S["tan"], 2)
            dve.wait_ge(S["wgt"], 3)
            dve.tensor_scalar(wg[:].rearrange("p k o -> p (k o)"), CV[0][:, 0:TAPS * P], gt[:, 0:1], None,
                              ALU.mult).then_inc(S["wgv"], 1)
            dve.tensor_scalar(gt[:, 5:6], gt[:, 4:5], 1.0, None, ALU.add).then_inc(S["tanv"], 1)
            dve.wait_ge(S["tanv"], 1)
            dve.reciprocal(gt[:, 2:3], gt[:, 5:6]).then_inc(S["tanv"], 1)
            dve.wait_ge(S["tanv"], 2)
            dve.tensor_scalar(gt[:, 3:4], gt[:, 2:3], -1.0, 1.0, ALU.mult, ALU.add).then_inc(S["tanv"], 1)
            dve.wait_ge(S["tanv"], 3)
            dve.wait_ge(S["wgv"], 1)

            def logit_weights():
                dve.wait_ge(S["wlt"], NCH)
                dve.tensor_copy(wl[:], XT[:, 64:64 + NCH * LP].rearrange("p (j l) -> p j l", j=NCH)
                                ).then_inc(S["wlc"], 1)

            def logit_weight_sums():
                dve.wait_ge(S["wlt"], NCH + 1)
                dve.tensor_copy(wsum[:], XT[:, 0:LP]).then_inc(S["wlc"], 1)

            def scale_x(b, h, k):
                s = b[1] % 2
                lo, hi = h * H, (h + 1) * H
                t0, t1 = max(lo, 1 - k), min(hi, T + 1 - k)
                if h == 0 and k == 0:
                    dve.wait_ge(S["mvx"], at(b, 1, 1))
                dve.wait_ge(S["att"], at(b, 6, 3 * h + k + 1))
                if reused(b, 1):
                    dve.wait_ge(S["conv"], at(b, 6, 3 * h + k + 1 - 6))
                dve.scalar_tensor_tensor(out=gs[k][:, t0:t1], in0=xs[s][:, t0 + k - 1:t1 + k - 1],
                                         scalar=nmean[s][:], in1=ATT[k][:, t0 - lo:t1 - lo],
                                         op0=ALU.add, op1=ALU.mult).then_inc(S["g"], 1)

            def invert_deviation(b):
                dve.wait_ge(S["sdx"], at(b, 1, 1))
                dve.reciprocal(rsx[:], sdx[:]).then_inc(S["rsx"], 1)

            sums = DM[:, :, 0:3 * P].rearrange("p r (d q m) -> p q r d m", d=3, q=4)

            def norms(b):
                dve.wait_ge(S["dT"], at(b, 1, 1))
                if reused(b, 1):
                    dve.wait_ge(S["nq"], at(b))
                dve.tensor_scalar(nm[:].rearrange("p (q r) m -> p q r m", r=2), sums[:, :, :, :, 0],
                                  COS_EPS * COS_EPS, None, ALU.max).then_inc(S["nm"], 1)

            def norms2(b):
                dve.wait_ge(S["nq"], at(b, 1, 1))
                dve.reciprocal(inv[:], nq[:]).then_inc(S["inv"], 1)

            def norms3(b):
                dve.wait_ge(S["inv"], at(b, 1, 1))
                dve.tensor_tensor(ww[:], inv[:], inv[:, :, 1:2].broadcast_to([P, NCH, 3]), ALU.mult
                                  ).then_inc(S["ww"], 1)

            def cosines(b):
                dve.wait_ge(S["ww"], at(b, 1, 1))
                if reused(b, 1):
                    dve.wait_ge(S["split"], at(b))
                wv = ww[:].rearrange("p (q r) m -> p q r m", r=2)
                sv = sims[:].rearrange("p (q r) m -> p q r m", r=2)
                dve.tensor_tensor(sv[:, :, :, 0:3:2], wv[:, :, :, 0:3:2], sums[:, :, :, 0:2, 1], ALU.mult
                                  ).then_inc(S["sims"], 1)
                dve.tensor_tensor(sv[:, :, :, 1], wv[:, :, :, 1], sums[:, :, :, 1, 0], ALU.mult
                                  ).then_inc(S["sims"], 1)

            def residual(b, h):
                s = b[1] % 2
                dve.wait_ge(S["conv"], at(b, 6, 3 * h + 3))
                if h == 0 and reused(b, 2):
                    dve.wait_ge(kept[s], at((b[0], b[1] // 2 * 2), 8))
                    dve.wait_ge(S["XT"], at(b, 2, -2))
                    dve.wait_ge(S["dev2"], at(b, 1, -1))
                dve.tensor_tensor(x2[s][:, h * H:(h + 1) * H], CV[h][:], xs[s][:, h * H:(h + 1) * H], ALU.add
                                  ).then_inc(S["x2"], 1)

            def step(t, beside=nothing):
                n, l = later(t, 1), later(t, -1)
                if exists(t, NB):
                    scale_x(t, 0, 0)
                beside(t, 0)
                if exists(t, NB):
                    scale_x(t, 0, 1)
                beside(t, 1)
                if exists(t, NB):
                    scale_x(t, 0, 2)
                beside(t, 2)
                beside(t, 3)
                if exists(t, NB):
                    scale_x(t, 1, 0)
                beside(t, 4)
                if exists(n, NB):
                    norms(n)
                beside(t, 5)
                if exists(t, NB):
                    scale_x(t, 1, 1)
                beside(t, 6)
                if exists(n, NB):
                    norms2(n)
                beside(t, 7)
                if exists(n, NB):
                    norms3(n)
                    cosines(n)
                if exists(t, NB):
                    scale_x(t, 1, 2)
                if first(t):
                    logit_weights()
                beside(t, 8)
                beside(t, 9)
                if exists(t, NB):
                    residual(t, 0)
                beside(t, 10)
                if exists(n, NB):
                    invert_deviation(n)
                beside(t, 11)
                beside(t, 12)
                beside(t, 13)
                if exists(t, NB):
                    residual(t, 1)
                for k in range(14, 20):
                    beside(t, k)
                if first(t):
                    logit_weight_sums()

            ch = [0]

            def link(ins):
                ch[0] += 1
                ins.then_inc(S["ch"], 1)
                dve.wait_ge(S["ch"], ch[0])

            def wide(a, hs, n):
                return a[:, hs].unsqueeze(2).broadcast_to([P, hs.stop - hs.start, n])

            def over_j(a, hs):
                return a[:, hs].unsqueeze(3).broadcast_to([P, hs.stop - hs.start, NS, NS])

            def over_i(a, hs):
                return a[:, hs].unsqueeze(2).broadcast_to([P, hs.stop - hs.start, NS, NS])

            c5 = coefs[:, :, 0:20].rearrange("p b (i j) -> p b i j", i=NS)

            def variances(e):
                hs = halves[e]
                dve.wait_ge(S["dev2"], hs.stop)
                dve.tensor_scalar(ve[:, hs], ssq2[:, hs], 1.0 / T, LN_EPS, ALU.mult, ALU.add
                                  ).then_inc(S["ve"], 1)
                link(dve.tensor_scalar(var[:, hs], ssq2[:, hs], 1.0 / T, None, ALU.mult))

            def squares(e):
                hs = halves[e]
                dve.wait_ge(S["rstd"], e + 1)
                link(dve.reciprocal(rstd[:, hs], rstd[:, hs]))
                link(dve.tensor_tensor(rms[:, hs], rstd[:, hs], rstd[:, hs], ALU.mult))
                link(dve.tensor_tensor(rms[:, hs], rms[:, hs], var[:, hs], ALU.mult))
                dve.tensor_scalar(rms[:, hs], rms[:, hs], RMS_EPS, None, ALU.add).then_inc(S["rms"], 1)

            def logits(e):
                hs = halves[e]
                shape = [P, HB, NL]
                link(dve.tensor_tensor(tmp[:, hs], wsum[:, 0:NL].unsqueeze(1).broadcast_to(shape),
                                       wide(nmean2, hs, NL), ALU.mult))
                dve.wait_ge(S["raw"], hs.stop)
                link(dve.tensor_tensor(tmp[:, hs], raw[:, hs, 0:NL], tmp[:, hs], ALU.add))
                dve.wait_ge(S["rs"], e + 1)
                link(dve.reciprocal(rs[:, hs], rs[:, hs]))
                link(dve.tensor_tensor(rs[:, hs], rs[:, hs], rstd[:, hs], ALU.mult))
                link(dve.tensor_tensor(tmp[:, hs], tmp[:, hs], wide(rs, hs, NL), ALU.mult))
                link(dve.tensor_tensor(logit[:, hs], tmp[:, hs], crow[:, 0:NL].unsqueeze(1).broadcast_to(shape),
                                       ALU.add))

            def exponents(e):
                hs = halves[e]
                zh, zmh = z[:, hs], zm[:, hs]
                link(dve.tensor_scalar(zh.rearrange("p b i j -> p b (i j)"), logit[:, hs, 0:16],
                                       1.0 / SINKHORN_TAU, None, ALU.mult))
                link(dve.tensor_reduce(zmh, zh, AX.X, ALU.max))
                link(dve.tensor_tensor(zh, zh, over_j(zm, hs), ALU.subtract))
                link(dve.tensor_reduce(zmh, zh.rearrange("p b i j -> p b j i"), AX.X, ALU.max))
                dve.tensor_tensor(zh, zh, over_i(zm, hs), ALU.subtract).then_inc(S["z"], 1)

            def setup(t, k):
                if k == 0:
                    variances(0)
                if k == 4:
                    squares(0)
                if k == 10:
                    logits(0)
                if k == 12:
                    exponents(0)

            def total(i, n, e):
                dve.wait_ge(prod[e], i * 2 + (n + 1))
                w = kt[:, chains[e]]
                dve.tensor_reduce(ssum[:, chains[e]], w.rearrange("p b i j -> p b j i") if n else w, AX.X,
                                  ALU.add).then_inc(sink[e], 1)

            def invert(i, n, e):
                dve.wait_ge(sink[e], i * 4 + (2 * n + 2))
                dve.reciprocal((av, bv)[n][:, chains[e]], ssum[:, chains[e]]).then_inc(sink[e], 1)

            def iterate_a(t, k):
                h = half_a(t, k // 2)
                if h:
                    (total, invert)[k % 2](*h, 0)

            def absorb(e):
                hs = halves[e]
                dve.wait_ge(S["lnab"], 2 * e + 2)
                link(dve.tensor_tensor(z[:, hs], z[:, hs], over_j(av, hs), ALU.add))
                dve.memset(bv[:, hs], 1.0).then_inc(S["ch"], 1)
                ch[0] += 1
                dve.tensor_tensor(z[:, hs], z[:, hs], over_i(ln_, hs), ALU.add).then_inc(S["z"], 1)

            def mix_coefficients(e):
                hs = halves[e]
                ah = aij[:, hs]
                a4 = ah.rearrange("p b (i j) -> p b i j", i=NS)
                if e == 0:
                    dve.wait_ge(sink[0], 1 + 4 * SINKHORN_ITERS)
                else:
                    dve.wait_ge(sink[2], 1 + 4 * HALFWAY)
                    dve.wait_ge(sink[3], 1 + 4 * HALFWAY)
                link(dve.tensor_tensor(kt[:, hs], kk[:, hs], over_j(av, hs), ALU.mult))
                link(dve.tensor_tensor(a4, kt[:, hs], over_i(bv, hs), ALU.mult))
                link(dve.tensor_scalar(ah, ah, gt[:, 2:3], None, ALU.mult))
                link(dve.tensor_scalar(aij[:, hs, 0:16:5], aij[:, hs, 0:16:5], gt[:, 3:4], None, ALU.add))
                link(dve.tensor_tensor(ah, ah, wide(rs, hs, 16), ALU.mult))
                link(dve.tensor_reduce(zm[:, hs], a4, AX.X, ALU.add))
                link(dve.tensor_tensor(coefs[:, hs, 24:28], zm[:, hs], wide(nmean2, hs, NS), ALU.mult))
                link(dve.tensor_copy(c5[:, hs, :, 0:NS], a4))
                dve.tensor_scalar(coefs[:, hs, 0:20:6], aij[:, hs, 0:16:5], 1.0, None, ALU.add
                                  ).then_inc(S["cmix"], 1)

            steps(dve, step, setup, iterate_a)

            every = slice(0, NB)
            variances(1)
            squares(1)
            logits(1)
            exponents(1)
            absorb(0)
            pp = logit[:, :, 16:24].rearrange("p b (w n) -> p b w n", w=2)
            link(dve.tensor_reduce(mx[:], pp, AX.X, ALU.max))
            dve.tensor_tensor(hpp[:], pp, mx[:].unsqueeze(3).broadcast_to([P, NB, 2, NS]), ALU.subtract
                              ).then_inc(S["pp"], 1)

            dve.wait_ge(S["hpp"], 1)
            link(dve.tensor_reduce(hsum[:], hpp[:], AX.X, ALU.add))
            total(HALFWAY, 0, 0)
            link(dve.reciprocal(hsum[:], hsum[:]))
            invert(HALFWAY, 0, 0)
            link(dve.tensor_tensor(hpp[:], hpp[:], hsum[:].unsqueeze(3).broadcast_to([P, NB, 2, NS]), ALU.mult))
            total(0, 0, 1)
            link(dve.tensor_tensor(coefs[:, :, 20:24], hpp[:, :, 0, :], wide(rstd, every, NS), ALU.mult))
            invert(0, 0, 1)
            link(dve.tensor_reduce(pbias[:], coefs[:, :, 20:24], AX.X, ALU.add))
            total(HALFWAY, 1, 0)
            dve.tensor_tensor(coefs[:, :, 28], pbias[:], nmean2[:], ALU.mult).then_inc(S["cpre"], 1)
            invert(HALFWAY, 1, 0)
            total(0, 1, 1)
            invert(0, 1, 1)
            with dve.Fori(1, HALFWAY, 4) as i:
                for u in range(4):
                    for n in range(2):
                        total(i + (HALFWAY + u), n, 0)
                        invert(i + (HALFWAY + u), n, 0)
                        total(i + u, n, 1)
                        invert(i + u, n, 1)
            link(dve.tensor_scalar(c5[:, :, :, NS], hpp[:, :, 1, :], gt[:, 1:2], None, ALU.mult))
            link(dve.tensor_scalar(rs[:], rstd[:], gt[:, 1:2], None, ALU.mult))
            absorb(1)
            mix_coefficients(0)

            def mix(b, i, j, count=1):
                if i > HS:
                    dve.wait_ge(S["mixo"], at(b, HS, 1))
                elif j == 1:
                    dve.wait_ge(S["som"], at(b, HS, i + 1))
                else:
                    dve.wait_ge(S["mixd"], at(b, MIXD, HS * (j - 2) + i + 1))
                if j == NS and i == 0:
                    dve.wait_ge(S["ysb"], at(b, 1, 1))
                o = out_of(b, i)
                src = x2_of(b, j) if j < NS else y_of(b)
                dve.scalar_tensor_tensor(out=o, in0=src, scalar=coef(b, (NS + 1) * i + j), in1=o,
                                         op0=ALU.mult, op1=ALU.add).then_inc(S["mixd"], count)

            def mstep(t, early):
                terms = [(i, j) for j in range(1, NS + 1) for i in range(HS)]
                if not early:
                    terms.append((HS + 1, NS))
                halves_here = sum(half_m(t, k) is not None for k in range(10)) if early else 0
                if early and not halves_here:
                    mix_coefficients(1)
                k = 0
                late = None
                for m, (i, j) in enumerate(terms):
                    mix(t, i, j, 2 if early and m == len(terms) - 1 else 1)
                    if late is not None:
                        for e in (2, 3):
                            invert(*half_m(t, late), e)
                        late = None
                    elif k < halves_here and k * len(terms) // halves_here <= m:
                        for e in (2, 3):
                            total(*half_m(t, k), e)
                        if (k + 1) * len(terms) // halves_here > m + 1 and m + 1 < len(terms):
                            late = k
                        else:
                            for e in (2, 3):
                                invert(*half_m(t, k), e)
                        k += 1
                assert k == halves_here and late is None

            for s in range(2):
                dve.wait_ge(kept[s], 16 * NB // 2)
            msteps(dve, mstep)

    return nc


_INS = ['x', 'ctx_4096', 'g_xattn', 'g_ffn', 'L0_xattn_weight', 'L0_ffn_W_res', 'L0_ffn_W_pre', 'L0_ffn_W_post',
        'L0_ffn_H_res_base', 'L0_ffn_H_pre_base', 'L0_ffn_H_post_base', 'L0_ffn_gate', 'L0_ffn_W_branch']
_OUTS = [((16, 128, 1024), 'float32')]


def kernel(**inputs):
    import numpy as _np
    import concourse.bacc as _bacc
    from concourse import mybir as _mybir
    from concourse.bass_utils import run_bass_kernel_spmd as _run

    nc = _bacc.Bacc("TRN2", target_bir_lowering=False, num_devices=1)
    arrays, args = {}, []
    for name in _INS:
        a = _np.ascontiguousarray(inputs[name])
        arrays[f"in_{name}_dram"] = a
        args.append(nc.dram_tensor(f"in_{name}_dram", a.shape, _mybir.dt.from_np(a.dtype), kind="ExternalInput").ap())
    for i, (shape, dtype) in enumerate(_OUTS):
        dt = _mybir.dt.from_np(_np.dtype(dtype))
        args.append(nc.dram_tensor(f"out_{i}_dram", shape, dt, kind="ExternalOutput").ap())
    build(nc, *args)
    r = _run(nc, [arrays], core_ids=[0])
    got = tuple(r.results[0][f"out_{i}_dram"] for i in range(len(_OUTS)))
    return got[0]
```
